# Optimizing a Trainium2 kernel written in Bass

```python
import numpy as np
import jax
import jax.numpy as jnp

def _softmax(x, axis=-1):
    return jax.nn.softmax(x, axis=axis)

def _gelu(x):
    return jax.nn.gelu(x, approximate=True)

def _silu(x):
    return jax.nn.silu(x)

def _sigmoid(x):
    return jax.nn.sigmoid(x)

def _layernorm(x, axis=-1, eps=1e-05):
    m = jnp.mean(x, axis=axis, keepdims=True)
    v = jnp.var(x, axis=axis, keepdims=True)
    return (x - m) / jnp.sqrt(v + eps)

def _scatter_add(tgt, idx, src, axis=0):
    return tgt.at[idx].add(src)

def _segment_sum(src, seg, n):
    return jax.ops.segment_sum(src, seg, n)
kernel_name = 'mk_recurrent_d1_jaxref_r4_bd9711'

def setup_inputs(seed: int=0):
    np.random.seed(seed)
    _w = jnp.asarray

    def _L0_attn_setup():
        import jax, jax.numpy as jnp
        import numpy as np
        BH = 32
        BW = 32
        key = jax.random.key(seed)
        k1, k2, k3, k4 = jax.random.split(key, 4)
        B, S, K, N = (2, 512, 1024, 1024)
        data = jax.random.normal(k1, (B, S, K), dtype=jnp.float32)
        weight = jax.random.normal(k2, (N, K), dtype=jnp.float32) * 0.02
        bias = jax.random.normal(k3, (N,), dtype=jnp.float32) * 0.02
        Nb, Kb = (N // BH, K // BW)
        block_on = jax.random.uniform(k4, (Nb, Kb)) < 0.3
        mask = jnp.repeat(jnp.repeat(block_on, BH, axis=0), BW, axis=1).astype(jnp.int32)
        return {'data': data, 'mask': mask, 'weight': weight, 'bias': bias}
    _L0_attn_in = _L0_attn_setup()

    def _L0_ffn_setup():
        import jax, jax.numpy as jnp
        import numpy as np
        import math
        B, S, IN, OUT = (4, 512, 1024, 1024)
        E, R, K = (8, 64, 128)
        SCALE = 64.0 / 64.0
        MULTIPLIER = 1.0
        key = jax.random.key(seed)
        ks = jax.random.split(key, 6)
        return {'x': jax.random.normal(ks[0], (B, S, IN), jnp.float32), 'W_org': jax.random.normal(ks[1], (OUT, IN), jnp.float32) * 0.02, 'lora_down': jax.random.normal(ks[2], (E, IN, R), jnp.float32) * 0.02, 'lora_up': jax.random.normal(ks[3], (E, R, OUT), jnp.float32) * 0.02, 'lora_keys': jax.random.normal(ks[4], (E, K), jnp.float32), 'Wq': jax.random.normal(ks[5], (K, IN), jnp.float32) * 0.02}
    _L0_ffn_in = _L0_ffn_setup()
    _d = {'L0_attn_data': _L0_attn_in['data'], 'L0_attn_mask': _L0_attn_in['mask'], 'L0_attn_weight': _L0_attn_in['weight'], 'L0_attn_bias': _L0_attn_in['bias'], 'L0_ffn_W_org': _L0_ffn_in['W_org'], 'L0_ffn_lora_down': _L0_ffn_in['lora_down'], 'L0_ffn_lora_up': _L0_ffn_in['lora_up'], 'L0_ffn_lora_keys': _L0_ffn_in['lora_keys'], 'L0_ffn_Wq': _L0_ffn_in['Wq']}
    _x0 = _d['L0_attn_data']
    _d['L0_attn_data'] = jax.random.normal(jax.random.fold_in(jax.random.key(seed), 1), (2, 1024, 1024), dtype=_x0.dtype)
    del _x0
    return _d

def reference(L0_attn_data, L0_attn_mask, L0_attn_weight, L0_attn_bias, L0_ffn_W_org, L0_ffn_lora_down, L0_ffn_lora_up, L0_ffn_lora_keys, L0_ffn_Wq):

    def _L0_attn_ref(data, mask, weight, bias):
        import jax, jax.numpy as jnp
        import numpy as np
        BH = 32
        BW = 32
        N, K = weight.shape
        Nb, Kb = (N // BH, K // BW)
        bm = mask.reshape(Nb, BH, Kb, BW).sum(axis=(1, 3)) > 0
        wb = weight.reshape(Nb, BH, Kb, BW) * bm[:, None, :, None].astype(weight.dtype)
        w = wb.reshape(N, K)
        out = jnp.einsum('bsk,nk->bsn', data, w) + bias
        return out

    def _L0_ffn_ref(x, W_org, lora_down, lora_up, lora_keys, Wq):
        import jax, jax.numpy as jnp
        import numpy as np
        import math
        B, S, IN, OUT = (4, 512, 1024, 1024)
        E, R, K = (8, 64, 128)
        SCALE = 64.0 / 64.0
        MULTIPLIER = 1.0
        base = jnp.einsum('bsi,oi->bso', x, W_org)
        q = jnp.einsum('bi,ki->bk', x.mean(axis=1), Wq)
        scores = jnp.einsum('bk,ek->be', q, lora_keys) / math.sqrt(K)
        coeffs = jax.nn.softmax(scores, axis=-1)
        h = jnp.einsum('bsi,eir->bser', x, lora_down)
        delta = jnp.einsum('be,bser,ero->bso', coeffs, h, lora_up)
        return base + delta * (SCALE * MULTIPLIER)
    x = L0_attn_data
    xn = _layernorm(x, axis=-1)
    s = _L0_attn_ref(xn, L0_attn_mask, L0_attn_weight, L0_attn_bias)
    g = _silu(_L0_ffn_ref(xn, L0_ffn_W_org, L0_ffn_lora_down, L0_ffn_lora_up, L0_ffn_lora_keys, L0_ffn_Wq))
    x = x + s * g
    return x

_drawn_inputs = setup_inputs


def setup_inputs(seed=0):
    import zlib

    import numpy as np

    out = dict(_drawn_inputs(seed))
    spreads = {}
    factors = {'L0_attn_bias': 8.0,
     'L0_ffn_lora_down': 8.0,
     'L0_ffn_lora_up': 8.0,
     'L0_ffn_lora_keys': 8.0,
     'L0_ffn_Wq': 8.0}
    for name, (base, spread) in spreads.items():
        noise = np.random.default_rng([zlib.crc32(name.encode()), seed]).standard_normal(out[name].shape)
        drawn = base * np.exp(spread * noise) if base else spread * noise
        out[name] = jnp.asarray(drawn.astype(out[name].dtype))
    for name, factor in factors.items():
        out[name] = (out[name] * factor).astype(out[name].dtype)
    return out
```

```python
from contextlib import ExitStack

import concourse.bass as bass
from concourse import mybir

P = 128
H = 512
F32 = mybir.dt.float32
F32R = mybir.dt.float32r
I32 = mybir.dt.int32
ALU = mybir.AluOpType
ACT = mybir.ActivationFunctionType
AX = mybir.AxisListType

XIN = 2
WST = 4
STG = 5
TRING = 6
SGR = 4
BLK = 32


def schedule():
    s = []

    def A(b, h, j):
        s.append(("A", b, h, j, 0))
        s.append(("A", b, h, j, 1))

    def load_updown(b, h):
        for t in range(4):
            s.append(("U", b, h, t))
        s.append(("D", b, h, 0))

    def make_E(b, h):
        for k in range(8):
            if k < 7:
                s.append(("D", b, h, k + 1))
            s.append(("L", b, h, k))

    s += [("X", 0, 0), ("M", 0, 0), ("T", 0, 0), ("M", 0, 1), ("W", 0, 0), ("X", 0, 1), ("M", 0, 2), ("W", 0, 1),
          ("M", 0, 3), ("W", 0, 2), ("W", 0, 3)]
    s += [("A", 0, 0, 0, 0), ("T", 0, 1), ("X", 0, 2), ("A", 0, 0, 0, 1), ("T", 0, 2), ("X", 0, 3),
          ("A", 0, 0, 1, 0), ("T", 0, 3), ("X", 0, 4), ("K",), ("A", 0, 0, 1, 1), ("T", 0, 4), ("X", 0, 5),
          ("Q", 0), ("Q", 1), ("A", 0, 0, 2, 0), ("T", 0, 5), ("X", 0, 6), ("A", 0, 0, 2, 1), ("T", 0, 6),
          ("X", 0, 7), ("M", 1, 0), ("A", 0, 0, 3, 0), ("T", 0, 7), ("M", 1, 1), ("W", 1, 0), ("A", 0, 0, 3, 1),
          ("C", 0), ("M", 1, 2), ("W", 1, 1), ("A", 0, 0, 4, 0), ("M", 1, 3), ("W", 1, 2)]
    load_updown(0, 0)
    s += [("W", 1, 3), ("A", 0, 0, 4, 1)]
    for b in range(2):
        if b:
            A(1, 0, 0)
            A(1, 0, 1)
            s.append(("C", 1))
            A(1, 0, 2)
            load_updown(1, 0)
            A(1, 0, 3)
        make_E(b, 0)
        first = 5 - b
        A(b, 0, first)
        s += [("B", b, 0, 0), ("B", b, 0, 1)]
        nxt = 2
        for j in range(first + 1, 8):
            A(b, 0, j)
            s.append(("B", b, 0, nxt))
            nxt += 1
        for j in range(nxt, 7):
            s.append(("B", b, 0, j))
        load_updown(b, 1)
        s.append(("B", b, 0, 7))
        make_E(b, 1)
        A(b, 1, 0)
        if b == 0:
            s.append(("X", 1, 0))
        for j in range(8):
            if j < 7:
                A(b, 1, j + 1)
            s.append(("B", b, 1, j))
            if b == 0:
                s.append(("T", 1, j))
                if j < 7:
                    s.append(("X", 1, j + 1))
    return s


def gated_block_linear_lora(nc, data, mask, weight, bias, w_org, down, up, keys, wq, out):
    NB, S, D = data.shape
    N = weight.shape[0]
    E, _, R = down.shape
    QD = keys.shape[1]
    NT, KC = S // P, D // P
    assert (NB, NT, KC, N, E * R, QD) == (2, 8, 8, 2 * H, H, P)
    EPS = 1e-5
    SCORE_SCALE = 1.0 / (S * float(QD) ** 0.5)

    steps = schedule()

    t_use, l_use, sg_use, stage_use, a_use = {}, {}, {}, {}, {}
    for st in steps:
        kind = st[0]
        if kind in "TW":
            for half in range(2):
                t_use[st + (half,)] = len(t_use)
        if kind == "D":
            t_use[st] = len(t_use)
        if kind in "MKQCL":
            l_use[st] = len(l_use)
        if kind == "A" and st[4] == 1:
            sg_use[st[:4]] = len(sg_use)
            a_use[st[:4]] = len(a_use)
        if kind == "B":
            sg_use[st] = len(sg_use)
        if kind == "K":
            stage_use[st] = len(stage_use)
        if kind in "QUDB":
            stage_use[st] = len(stage_use)
        if kind == "L":
            stage_use[st] = len(stage_use)
    order = []
    for st in steps:
        if st[0] == "A" and st[4] == 0:
            order.append(st[:4])
        if st[0] == "B":
            order.append(st)
    assert order == sorted(order, key=lambda k: sg_use[k])
    x_use = {st: n for n, st in enumerate(s for s in steps if s[0] == "X")}
    w_use = {st: n for n, st in enumerate(s for s in steps if s[0] == "M")}
    u_use = {st: n for n, st in enumerate(s for s in steps if s[0] == "U")}
    b_use = {st: n for n, st in enumerate(s for s in steps if s[0] == "B")}

    x_v = data.rearrange("b (j p) k -> b j p k", p=P)
    out_v = out.rearrange("b (j p) n -> b j p n", p=P)
    w_v = weight.rearrange("(h n p) k -> h n p k", p=P, h=2)
    mask_v = mask.rearrange("(h n p) k -> h n p k", p=P, h=2)
    worg_v = w_org.rearrange("(h n p) i -> h p n i", p=P, h=2)
    down_v = down.rearrange("e i r -> i e r")
    up_v = up.rearrange("e r o -> (e r) o")

    ctx = ExitStack()
    with ctx:
        def sb(name, shape, dt=F32):
            return ctx.enter_context(nc.sbuf_tensor(name, shape, dt))

        def sem(name):
            return ctx.enter_context(nc.semaphore(name))

        ident = sb("ident", [P, P])
        blk_ones = sb("blk_ones", [P, P])
        ones = sb("ones", [P, P])
        bias_bc = sb("bias_bc", [P, N])
        xT_hi = sb("xT_hi", [P, NT, KC, P], F32R)
        xT_lo = sb("xT_lo", [P, NT, KC, P], F32R)
        wT_hi = sb("wT_hi", [P, KC, N], F32R)
        wT_lo = sb("wT_lo", [P, KC, N], F32R)
        up_hi = sb("up_hi", [P, 4, H], F32R)
        up_lo = sb("up_lo", [P, 4, H], F32R)
        dT_hi = sb("dT_hi", [P, 2, 4, P], F32R)
        dT_lo = sb("dT_lo", [P, 2, 4, P], F32R)
        xin = sb("xin", [P, XIN, D])
        stage = sb("stage", [P, STG, H])
        t_out = sb("t_out", [P, TRING, H])
        stats = sb("stats", [P, XIN, 2, 6])
        mv = sb("mv", [P, XIN, 2])
        rstd = sb("rstd", [P, XIN])
        neg_half = sb("neg_half", [P, 1])
        rowcnt = sb("rowcnt", [P, 2, N // BLK])
        bmask = sb("bmask", [P, 2, N // BLK])
        xpart = sb("xpart", [P, KC, NT])
        xsum = sb("xsum", [P, KC])
        keysT = sb("keysT", [P, E])
        kq = sb("kq", [P, E, KC])
        kqx = sb("kqx", [P, E, KC])
        kqs = sb("kqs", [P, E])
        nmax = sb("nmax", [P, 2])
        expo = sb("expo", [P, E])
        esum = sb("esum", [P, 2])
        coef = sb("coef", [P, 4])
        with nc.sbuf_tensor("w_stage", [P, WST, D], F32) as w_stage, \
                nc.sbuf_tensor("m_stage", [P, WST, D], I32) as m_stage:
            pass
        e_hi = sb("e_hi", [P, KC, H], F32R)
        e_lo = sb("e_lo", [P, KC, H], F32R)

        psT = ctx.enter_context(nc.psum_tensor("psT", [P, 2, H], F32))
        psL = ctx.enter_context(nc.psum_tensor("psL", [P, 2, H], F32))
        psSG = ctx.enter_context(nc.psum_tensor("psSG", [P, SGR, H], F32))

        x_loaded = [sem(f"x_loaded{i}") for i in range(XIN)]
        w_loaded = [sem(f"w_loaded{i}") for i in range(WST)]
        m_loaded = [sem(f"m_loaded{i}") for i in range(WST)]
        stage_loaded = [sem(f"stage_loaded{i}") for i in range(STG)]
        stored = [sem(f"stored{i}") for i in range(TRING)]
        bias_loaded = sem("bias_loaded")
        consts_zeroed = sem("consts_zeroed")
        consts_ready = sem("consts_ready")
        pe_T = sem("pe_T")
        pe_L = sem("pe_L")
        pe_SG = sem("pe_SG")
        act_T = sem("act_T")
        act_L = sem("act_L")
        act_exp = sem("act_exp")
        act_silu = sem("act_silu")
        act_U = sem("act_U")
        dve_T = sem("dve_T")
        dve_L = sem("dve_L")
        dve_SG = sem("dve_SG")
        dve_U = sem("dve_U")
        dve_var = sem("dve_var")
        dve_xn = sem("dve_xn")
        dve_cnt = sem("dve_cnt")
        dve_kq = sem("dve_kq")
        dve_max = sem("dve_max")
        dve_coef = sem("dve_coef")
        dve_own = sem("dve_own")
        pool_rstd = sem("pool_rstd")
        pool_w = sem("pool_w")
        pool_out = sem("pool_out")

        block = ctx.enter_context(nc.Block())

        def stage_slot(st):
            return stage[:, stage_use[st] % STG, :]

        def wait_stage(eng, st):
            n = stage_use[st]
            eng.wait_ge(stage_loaded[n % STG], 16 * (n // STG + 1))

        @block.sync
        def _(sp):
            by_stage = {n: st for st, n in stage_use.items()}

            def wait_stage_free(n):
                if n < STG:
                    return
                st = by_stage[n - STG]
                if st[0] in "KQL":
                    sp.wait_ge(pe_L, l_use[st] + 1)
                elif st[0] == "D":
                    sp.wait_ge(pe_T, t_use[st] + 1)
                elif st[0] == "U":
                    sp.wait_ge(dve_U, u_use[st] + 1)
                else:
                    sp.wait_ge(pool_out, b_use[st] + 1)

            def load_small(st, dst, src):
                n = stage_use[st]
                wait_stage_free(n)
                sp.dma_start(dst, src).then_inc(stage_loaded[n % STG], 16)

            def load(st):
                kind = st[0]
                if kind == "X":
                    _, b, j = st
                    n = x_use[st]
                    if n >= XIN:
                        sp.wait_ge(pe_T, t_use[("T", (n - XIN) // NT, (n - XIN) % NT, 1)] + 1)
                    sp.dma_start(xin[:, n % XIN, :], x_v[b, j]).then_inc(x_loaded[n % XIN], 16)
                elif kind == "M":
                    _, h, nt = st
                    n = w_use[st]
                    if n >= WST:
                        sp.wait_ge(pe_T, t_use[("W", (n - WST) // 4, (n - WST) % 4, 1)] + 1)
                    sp.dma_start(m_stage[:, n % WST, :], mask_v[h, nt]).then_inc(m_loaded[n % WST], 16)
                    sp.dma_start(w_stage[:, n % WST, :], w_v[h, nt]).then_inc(w_loaded[n % WST], 16)
                elif kind == "K":
                    load_small(st, stage_slot(st)[0:E, 0:QD], keys[:, :])
                    sp.dma_start(bias_bc[:, :], bias.rearrange("(o n) -> o n", o=1).to_broadcast([P, N]))\
                      .then_inc(bias_loaded, 16)
                elif kind == "Q":
                    load_small(st, stage_slot(st), wq[:, st[1] * H:(st[1] + 1) * H])
                elif kind == "U":
                    _, b, h, t = st
                    load_small(st, stage_slot(st), up_v[t * P:(t + 1) * P, h * H:(h + 1) * H])
                elif kind == "D":
                    k = st[3]
                    load_small(st, stage_slot(st).rearrange("p (e r) -> p e r", e=E), down_v[k * P:(k + 1) * P])
                elif kind == "L":
                    _, b, h, k = st
                    load_small(st, stage_slot(st).rearrange("p (n i) -> p n i", n=4),
                               worg_v[h, :, :, k * P:(k + 1) * P])
                elif kind == "B":
                    _, b, h, j = st
                    load_small(st, stage_slot(st), x_v[b, j, :, h * H:(h + 1) * H])

            def store(st):
                _, b, h, j = st
                n = a_use[("A", b, h, j)]
                sp.wait_ge(pool_out, b_use[st] + 1)
                sp.dma_start(out_v[b, j, :, h * H:(h + 1) * H], t_out[:, n % TRING, :])\
                  .then_inc(stored[n % TRING], 16)

            loads = [st for st in steps if st[0] in "XMKQUDLB"]
            AHEAD = 4
            for i, st in enumerate(loads):
                load(st)
                if i >= AHEAD and loads[i - AHEAD][0] == "B":
                    store(loads[i - AHEAD])
            for st in loads[-AHEAD:]:
                if st[0] == "B":
                    store(st)
            for i in range(TRING):
                uses = len([n for n in a_use.values() if n % TRING == i])
                sp.wait_ge(stored[i], 16 * uses)

        @block.tensor
        def _(pe):
            def product(ps, hi_l, lo_l, hi_r, lo_r, first, last):
                nc.tensor.matmul(ps, hi_l, hi_r, start=first, stop=False)
                nc.tensor.matmul(ps, hi_l, lo_r, start=False, stop=False)
                return nc.tensor.matmul(ps, lo_l, hi_r, start=False, stop=last)

            def transpose(ps, src, idn, first, last):
                return nc.tensor.matmul(ps, src, idn, start=first, stop=last, is_transpose=True)

            def take_T(n):
                if n >= 2:
                    pe.wait_ge(dve_T, n - 1)
                return psT[:, n % 2, :]

            def take_L(n):
                if n >= 2:
                    pe.wait_ge(dve_L, n - 1)
                return psL[:, n % 2, :]

            def take_SG(n):
                if n >= SGR:
                    pe.wait_ge(dve_SG, n - SGR + 1)
                return psSG[:, n % SGR, :]

            def four_transposes(n, src):
                bank = take_T(n)
                for q in range(4):
                    ins = transpose(bank[:, q * P:(q + 1) * P], src(q), ident[:, :], True, True)
                ins.then_inc(pe_T, 1)

            pe.wait_ge(consts_ready, 3)
            for st in steps:
                kind = st[0]
                if kind == "T":
                    _, b, j = st
                    n = x_use[("X", b, j)]
                    pe.wait_ge(dve_xn, n + 1)
                    for half in range(2):
                        four_transposes(t_use[st + (half,)],
                                        lambda q: xin[:, n % XIN, (4 * half + q) * P:(4 * half + q + 1) * P])
                elif kind == "M":
                    n, w = l_use[st], w_use[st]
                    bank = take_L(n)
                    pe.wait_ge(dve_cnt, w + 1)
                    nc.tensor.matmul(bank[:, 0:N // BLK], blk_ones[:, :], rowcnt[:, w % 2, :], start=True, stop=True)\
                        .then_inc(pe_L, 1)
                elif kind == "W":
                    _, h, nt = st
                    w = w_use[("M", h, nt)]
                    pe.wait_ge(pool_w, w + 1)
                    for half in range(2):
                        four_transposes(t_use[st + (half,)],
                                        lambda q: w_stage[:, w % WST, (4 * half + q) * P:(4 * half + q + 1) * P])
                elif kind == "K":
                    n = l_use[st]
                    bank = take_L(n)
                    wait_stage(pe, st)
                    transpose(bank[:, 0:E], stage_slot(st)[0:E, 0:QD], ident[0:E, 0:E], True, True).then_inc(pe_L, 1)
                elif kind == "Q":
                    n = l_use[st]
                    bank = take_L(n)
                    wait_stage(pe, st)
                    pe.wait_ge(dve_L, l_use[("K",)] + 1)
                    for q in range(4):
                        ins = nc.tensor.matmul(bank[:, q * E:(q + 1) * E], stage_slot(st)[:, q * P:(q + 1) * P],
                                               keysT[:, :], start=True, stop=True)
                    ins.then_inc(pe_L, 1)
                elif kind == "A":
                    _, b, h, j, part = st
                    n = sg_use[st[:4]]
                    if part == 0:
                        bank = take_SG(n)
                        pe.wait_ge(dve_T, t_use[("T", b, j, 1)] + 1)
                        if b == 0 and j == 0:
                            pe.wait_ge(dve_T, t_use[("W", h, 3, 1)] + 1)
                    bank = psSG[:, n % SGR, :]
                    for k in range(4 * part, 4 * part + 4):
                        ins = product(bank, xT_hi[:, j, k, :], xT_lo[:, j, k, :], wT_hi[:, k, h * H:(h + 1) * H],
                                      wT_lo[:, k, h * H:(h + 1) * H], k == 0, k == KC - 1)
                    if part == 1:
                        ins.then_inc(pe_SG, 1)
                elif kind == "B":
                    _, b, h, j = st
                    n = sg_use[st]
                    bank = take_SG(n)
                    pe.wait_ge(dve_L, l_use[("L", b, h, KC - 1)] + 1)
                    for k in range(KC):
                        ins = product(bank, xT_hi[:, j, k, :], xT_lo[:, j, k, :], e_hi[:, k, :], e_lo[:, k, :],
                                      k == 0, k == KC - 1)
                    ins.then_inc(pe_SG, 1)
                elif kind == "C":
                    n = l_use[st]
                    bank = take_L(n)
                    pe.wait_ge(dve_kq, st[1] + 1)
                    nc.tensor.matmul(bank[:, 0:E], ones[:, :], kqs[:, :], start=True, stop=True).then_inc(pe_L, 1)
                elif kind == "D":
                    wait_stage(pe, st)
                    four_transposes(t_use[st], lambda q: stage_slot(st)[:, q * P:(q + 1) * P])
                elif kind == "L":
                    _, b, h, k = st
                    n = l_use[st]
                    bank = take_L(n)
                    wait_stage(pe, st)
                    for q in range(4):
                        transpose(bank[:, q * P:(q + 1) * P], stage_slot(st)[:, q * P:(q + 1) * P], ident[:, :],
                                  q == 0, False)
                    if k == 0:
                        pe.wait_ge(dve_U, u_use[("U", b, h, 3)] + 1)
                    pe.wait_ge(dve_T, t_use[("D", b, h, k)] + 1)
                    for t in range(4):
                        ins = product(bank, dT_hi[:, k % 2, t, :], dT_lo[:, k % 2, t, :], up_hi[:, t, :],
                                      up_lo[:, t, :], False, t == 3)
                    ins.then_inc(pe_L, 1)

        def split_target(st, half):
            if st[0] == "T":
                ks = slice(4 * half, 4 * half + 4)
                return xT_hi[:, st[2], ks, :], xT_lo[:, st[2], ks, :]
            if st[0] == "W":
                ks, c = slice(4 * half, 4 * half + 4), (4 * st[1] + st[2]) * P
                return wT_hi[:, ks, c:c + P], wT_lo[:, ks, c:c + P]
            return dT_hi[:, st[3] % 2], dT_lo[:, st[3] % 2]

        def psT_blocks(n):
            return psT[:, n % 2, :].rearrange("p (q c) -> p q c", q=4)

        @block.scalar
        def _(act):
            for st in steps:
                kind = st[0]
                if kind in "TW":
                    for half in range(2):
                        n = t_use[st + (half,)]
                        if kind == "T" and st[1] == 1 and half == 0:
                            act.wait_ge(pe_SG, sg_use[("B", 0, 1, st[2])] + 1)
                        act.wait_ge(pe_T, n + 1)
                        nc.scalar.activation(split_target(st, half)[0], psT_blocks(n), ACT.Copy).then_inc(act_T, 1)
                elif kind == "D":
                    _, b, h, k = st
                    n = t_use[st]
                    if k >= 2:
                        act.wait_ge(pe_L, l_use[("L", b, h, k - 2)] + 1)
                    act.wait_ge(pe_T, n + 1)
                    nc.scalar.activation(split_target(st, 0)[0], psT_blocks(n), ACT.Copy).then_inc(act_T, 1)
                elif kind == "U":
                    _, b, h, t = st
                    if t == 0:
                        act.wait_ge(dve_coef, b + 1)
                        if (b, h) != (0, 0):
                            act.wait_ge(pe_L, l_use[("L", (2 * b + h - 1) // 2, (2 * b + h - 1) % 2, KC - 1)] + 1)
                    wait_stage(act, st)
                    nc.scalar.activation(up_hi[:, t, :], stage_slot(st), ACT.Copy, scale=coef[:, t:t + 1])\
                        .then_inc(act_U, 1)
                elif kind == "L":
                    _, b, h, k = st
                    n = l_use[st]
                    act.wait_ge(pe_L, n + 1)
                    nc.scalar.activation(e_hi[:, k, :], psL[:, n % 2, :], ACT.Copy).then_inc(act_L, 1)
                elif kind == "C":
                    act.wait_ge(dve_max, st[1] + 1)
                    nc.scalar.activation(expo[:, :], psL[:, l_use[st] % 2, 0:E], ACT.Exp, bias=nmax[:, 1:2],
                                         scale=SCORE_SCALE, accum_out=esum[:, 0:1]).then_inc(act_exp, 1)
                elif kind == "B":
                    n = sg_use[st]
                    act.wait_ge(pe_SG, n + 1)
                    nc.scalar.activation(psSG[:, n % SGR, :], psSG[:, n % SGR, :], ACT.Silu).then_inc(act_silu, 1)

        @block.vector
        def _(dve):
            own = [0]

            def mine(ins):
                own[0] += 1
                ins.then_inc(dve_own, 1)
                dve.wait_ge(dve_own, own[0])

            l_seen = [0]
            for st in steps:
                kind = st[0]
                if kind == "X":
                    n = x_use[st]
                    s = n % XIN
                    dve.wait_ge(x_loaded[s], 16 * (n // XIN + 1))
                    for half in range(2):
                        ins = nc.vector.bn_stats(stats[:, s, half, :], xin[:, s, half * H:(half + 1) * H])
                    mine(ins)
                    mine(nc.vector.bn_aggr(mv[:, s, :], stats[:, s, :, :]))
                    nc.vector.tensor_scalar(rstd[:, s:s + 1], mv[:, s, 1:2], EPS, None, ALU.add).then_inc(dve_var, 1)
                    dve.wait_ge(pool_rstd, n + 1)
                    nc.vector.tensor_scalar(xin[:, s, :], xin[:, s, :], mv[:, s, 0:1], rstd[:, s:s + 1],
                                            ALU.subtract, ALU.mult).then_inc(dve_xn, 1)
                elif kind in "TWD":
                    for half in range(1 if kind == "D" else 2):
                        n = t_use[st if kind == "D" else st + (half,)]
                        hi, lo = split_target(st, half)
                        dve.wait_ge(act_T, n + 1)
                        ins = nc.vector.tensor_tensor(lo, psT_blocks(n), hi.bitcast(F32), ALU.subtract)
                        if kind == "T":
                            ins = nc.vector.tensor_reduce(xpart[:, 4 * half:4 * half + 4, st[2]], psT_blocks(n),
                                                          AX.X, ALU.add)
                        ins.then_inc(dve_T, 1)
                elif kind == "M":
                    n, w = l_use[st], w_use[st]
                    dve.wait_ge(m_loaded[w % WST], 16 * (w // WST + 1))
                    nc.vector.tensor_reduce(rowcnt[:, w % 2, :],
                                            m_stage[:, w % WST, :].rearrange("p (c k) -> p c k", k=BLK),
                                            AX.X, ALU.add).then_inc(dve_cnt, 1)
                    if w >= 2:
                        dve.wait_ge(pool_w, w - 1)
                    dve.wait_ge(pe_L, n + 1)
                    nc.vector.tensor_scalar(bmask[:, w % 2, :], psL[:, n % 2, 0:N // BLK], 0.0, None, ALU.is_gt)\
                        .then_inc(dve_L, 1)
                elif kind == "K":
                    n = l_use[st]
                    dve.wait_ge(pe_L, n + 1)
                    nc.vector.tensor_copy(keysT[:, :], psL[:, n % 2, 0:E]).then_inc(dve_L, 1)
                elif kind == "Q":
                    n = l_use[st]
                    dve.wait_ge(pe_L, n + 1)
                    nc.vector.tensor_copy(kq[:, :, 4 * st[1]:4 * st[1] + 4].rearrange("p e q -> p q e"),
                                          psL[:, n % 2, 0:4 * E].rearrange("p (q e) -> p q e", q=4))\
                        .then_inc(dve_L, 1)
                elif kind == "C":
                    b, n = st[1], l_use[st]
                    dve.wait_ge(dve_T, t_use[("T", b, NT - 1, 1)] + 1)
                    dve.wait_ge(dve_L, l_use[("Q", 1)] + 1)
                    mine(nc.vector.tensor_reduce(xsum[:, :], xpart[:, :, :], AX.X, ALU.add))
                    mine(nc.vector.tensor_tensor(kqx[:, :, :], kq[:, :, :],
                                                 xsum[:, :].rearrange("p (o k) -> p o k", o=1).to_broadcast([P, E, KC]),
                                                 ALU.mult))
                    nc.vector.tensor_reduce(kqs[:, :], kqx[:, :, :], AX.X, ALU.add).then_inc(dve_kq, 1)
                    dve.wait_ge(pe_L, n + 1)
                    mine(nc.vector.tensor_reduce(nmax[:, 0:1], psL[:, n % 2, 0:E], AX.X, ALU.max))
                    nc.vector.tensor_scalar(nmax[:, 1:2], nmax[:, 0:1], -SCORE_SCALE, None, ALU.mult)\
                        .then_inc(dve_max, 1)
                    dve.wait_ge(act_exp, b + 1)
                    mine(nc.vector.reciprocal(esum[:, 1:2], esum[:, 0:1]))
                    if b:
                        dve.wait_ge(act_U, u_use[("U", b - 1, 1, 3)] + 1)
                    pairs = expo[:, :].rearrange("p (t two) -> p two t", two=2)
                    for half in range(2):
                        rows = slice(half * R, (half + 1) * R)
                        nc.vector.tensor_scalar(coef[rows, :], pairs[rows, half, :], esum[rows, 1:2], None, ALU.mult)\
                            .then_inc(dve_coef if half else dve_L, 1)
                elif kind == "U":
                    _, b, h, t = st
                    dve.wait_ge(act_U, u_use[st] + 1)
                    nc.vector.scalar_tensor_tensor(up_lo[:, t, :], stage_slot(st), coef[:, t:t + 1],
                                                   up_hi[:, t, :].bitcast(F32), ALU.mult, ALU.subtract)\
                        .then_inc(dve_U, 1)
                elif kind == "L":
                    _, b, h, k = st
                    n = l_use[st]
                    l_seen[0] += 1
                    dve.wait_ge(act_L, l_seen[0])
                    nc.vector.tensor_tensor(e_lo[:, k, :], psL[:, n % 2, :], e_hi[:, k, :].bitcast(F32), ALU.subtract)\
                        .then_inc(dve_L, 1)
                elif kind == "A" and st[4] == 1:
                    _, b, h, j, _ = st
                    n, a = sg_use[st[:4]], a_use[st[:4]]
                    if a == 0:
                        dve.wait_ge(bias_loaded, 16)
                    if a >= TRING:
                        dve.wait_ge(stored[a % TRING], 16 * (a // TRING))
                    dve.wait_ge(pe_SG, n + 1)
                    nc.vector.tensor_tensor(t_out[:, a % TRING, :], psSG[:, n % SGR, :],
                                            bias_bc[:, h * H:(h + 1) * H], ALU.add).then_inc(dve_SG, 1)
                elif kind == "B":
                    _, b, h, j = st
                    n, a = sg_use[st], a_use[("A", b, h, j)]
                    dve.wait_ge(dve_SG, sg_use[("A", b, h, j)] + 1)
                    dve.wait_ge(act_silu, b_use[st] + 1)
                    nc.vector.tensor_tensor(t_out[:, a % TRING, :], t_out[:, a % TRING, :], psSG[:, n % SGR, :],
                                            ALU.mult).then_inc(dve_SG, 1)

        @block.gpsimd
        def _(pool):
            nc.gpsimd.memset(neg_half[:, :], -0.5).then_inc(consts_zeroed, 1)
            nc.gpsimd.memset(ident[:, :], 0.0).then_inc(consts_zeroed, 1)
            nc.gpsimd.memset(blk_ones[:, :], 1.0).then_inc(consts_zeroed, 1)
            nc.gpsimd.memset(ones[:, :], 1.0).then_inc(consts_ready, 1)
            pool.wait_ge(consts_zeroed, 3)
            nc.gpsimd.affine_select(out=ident[:, :], in_=ident[:, :], compare_op=ALU.not_equal, fill=1.0,
                                    base=0, pattern=[[-1, P]], channel_multiplier=1).then_inc(consts_ready, 1)
            v = blk_ones[:, :].rearrange("p (g c) -> p g c", c=BLK)
            nc.gpsimd.affine_select(out=v, in_=v, compare_op=ALU.is_ge, fill=0.0, base=0,
                                    pattern=[[-BLK, P // BLK], [0, BLK]], channel_multiplier=1)\
                .then_inc(consts_zeroed, 1)
            pool.wait_ge(consts_zeroed, 4)
            nc.gpsimd.affine_select(out=v, in_=v, compare_op=ALU.is_ge, fill=0.0, base=BLK - 1,
                                    pattern=[[BLK, P // BLK], [0, BLK]], channel_multiplier=-1)\
                .then_inc(consts_ready, 1)
            for st in steps:
                kind = st[0]
                if kind == "X":
                    n = x_use[st]
                    s = n % XIN
                    pool.wait_ge(dve_var, n + 1)
                    nc.gpsimd.tensor_tensor(rstd[:, s:s + 1], rstd[:, s:s + 1], neg_half[:, :], ALU.pow)\
                        .then_inc(pool_rstd, 1)
                elif kind == "M":
                    w = w_use[st]
                    tile = w_stage[:, w % WST, :].rearrange("p (c k) -> p c k", k=BLK)
                    m = bmask[:, w % 2, :].rearrange("p (c o) -> p c o", o=1).to_broadcast([P, N // BLK, BLK])
                    pool.wait_ge(w_loaded[w % WST], 16 * (w // WST + 1))
                    pool.wait_ge(dve_L, l_use[st] + 1)
                    nc.gpsimd.tensor_tensor(tile, tile, m, ALU.mult).then_inc(pool_w, 1)
                elif kind == "B":
                    _, b, h, j = st
                    a = a_use[("A", b, h, j)]
                    wait_stage(pool, st)
                    pool.wait_ge(dve_SG, sg_use[st] + 1)
                    nc.gpsimd.tensor_tensor(t_out[:, a % TRING, :], t_out[:, a % TRING, :], stage_slot(st), ALU.add)\
                        .then_inc(pool_out, 1)


_INS = ["L0_attn_data", "L0_attn_mask", "L0_attn_weight", "L0_attn_bias", "L0_ffn_W_org", "L0_ffn_lora_down",
        "L0_ffn_lora_up", "L0_ffn_lora_keys", "L0_ffn_Wq"]


def kernel(**inputs):
    import numpy as _np
    import concourse.bacc as _bacc
    from concourse import mybir as _mybir
    from concourse.bass_utils import run_bass_kernel_spmd as _run

    nc = _bacc.Bacc("TRN2", target_bir_lowering=False, num_devices=1, dynamic_dma_scratch_size=1024)
    arrays, args = {}, []
    for name in _INS:
        a = _np.ascontiguousarray(inputs[name])
        arrays[f"in_{name}_dram"] = a
        args.append(nc.dram_tensor(f"in_{name}_dram", a.shape, _mybir.dt.from_np(a.dtype), kind="ExternalInput").ap())
    shape = inputs["L0_attn_data"].shape
    args.append(nc.dram_tensor("out_dram", shape, F32, kind="ExternalOutput").ap())
    gated_block_linear_lora(nc, *args)
    r = _run(nc, [arrays], core_ids=[0])
    return r.results[0]["out_dram"]
```

```python
from contextlib import ExitStack

import concourse.bass as bass
from concourse import mybir

P = 128
H = 512
F32 = mybir.dt.float32
F32R = mybir.dt.float32r
I32 = mybir.dt.int32
ALU = mybir.AluOpType
ACT = mybir.ActivationFunctionType
AX = mybir.AxisListType

XIN = 2
WST = 4
STAT = 4
STG = 3
RES = 3
TRING = 6
TR = 4
SGR = 2
BLK = 32


def schedule():
    def A(b, h, j):
        return [("A", b, h, j, 0), ("A", b, h, j, 1)]

    def up_and_first_down(b, h):
        return [("D", b, h, 0)] + [("U", b, h, t) for t in range(4)]

    def make_E(b, h):
        s = []
        for k in range(8):
            if k < 7:
                s.append(("D", b, h, k + 1))
            s.append(("L", b, h, k))
        return s

    s = [("X", 0, 0), ("Y", 0, 0), ("R", 0, 0), ("M", 0, 0), ("N", 0, 0), ("V", 0, 0), ("P", "T", 0, 0),
         ("R", 0, 1), ("M", 0, 1), ("N", 0, 1), ("V", 0, 1), ("T", 0, 0), ("P", "W", 0, 0),
         ("R", 0, 2), ("M", 0, 2), ("P", "W", 0, 1), ("R", 0, 3), ("M", 0, 3), ("N", 0, 2), ("V", 0, 2),
         ("W", 0, 0), ("N", 0, 3), ("V", 0, 3), ("W", 0, 1), ("W", 0, 2), ("W", 0, 3),
         ("X", 0, 1), ("Y", 0, 1), ("X", 0, 2), ("Y", 0, 2)]
    pre = A(0, 0, 0) + A(0, 0, 1) + A(0, 0, 2) + A(0, 0, 3) + A(0, 0, 4)
    for j in range(1, 8):
        s += [pre.pop(0), ("T", 0, j)]
        s += [("X", 0, j + 2)] if j + 2 < 8 else []
        s += [("Y", 0, j + 2)] if j + 2 < 8 else []
        s += {3: [("K",)], 5: [("Q", 0)], 6: [("Q", 1)]}.get(j, [])
    s += [pre.pop(0), ("C", 0), pre.pop(0), ("G", 0)] + up_and_first_down(0, 0) + [pre.pop(0)]
    s += make_E(0, 0)
    groups = [A(0, 0, 5), [("B", 0, 0, 0)], [("B", 0, 0, 1)], A(0, 0, 6), [("B", 0, 0, 2)], A(0, 0, 7),
              [("B", 0, 0, 3)], [("B", 0, 0, 4)], [("B", 0, 0, 5)], [("B", 0, 0, 6)]]
    s.append(("R", 1, 0))
    for i, g in enumerate(groups):
        n = i // 2
        s += g
        if i < 8 and i % 2 == 0:
            s += [("M", 1, n), ("N", 1, n), ("V", 1, n)]
        elif i < 8:
            s += [("W", 1, n)] + ([("R", 1, n + 1)] if n < 3 else [])
    for b in range(2):
        if b:
            s += A(1, 0, 0) + [("C", 1)] + A(1, 0, 1) + [("G", 1)] + A(1, 0, 2) + up_and_first_down(1, 0)
            s += A(1, 0, 3)
            s += make_E(1, 0) + A(1, 0, 4) + [("B", 1, 0, 0), ("B", 1, 0, 1)]
            for j in range(5, 8):
                s += A(1, 0, j) + [("B", 1, 0, j - 3)]
            s += [("B", 1, 0, 5), ("B", 1, 0, 6)]
        s += up_and_first_down(b, 1) + [("B", b, 0, 7)] + make_E(b, 1) + A(b, 1, 0)
        if b == 0:
            s += [("X", 1, 0), ("Y", 1, 0)]
        for j in range(8):
            s += A(b, 1, j + 1) if j < 7 else []
            s += [("B", b, 1, j)] if (b, j) != (1, 7) else [("B", 1, 1, 7, 0), ("B", 1, 1, 7, 1)]
            if b == 0:
                s += [("X", 1, j + 1), ("Y", 1, j + 1)] if j < 7 else []
                s.append(("T", 1, j))
    return s


def gated_block_linear_lora(nc, data, mask, weight, bias, w_org, down, up, keys, wq, out):
    NB, S, D = data.shape
    N = weight.shape[0]
    E, _, R = down.shape
    QD = keys.shape[1]
    NT, KC = S // P, D // P
    assert (NB, NT, KC, N, E * R, QD) == (2, 8, 8, 2 * H, H, P)
    EPS = 1e-5
    SCORE_SCALE = 1.0 / (S * float(QD) ** 0.5)

    steps = schedule()

    def number(keys):
        return {key: n for n, key in enumerate(keys)}

    def kinds(letters):
        return [st for st in steps if st[0] in letters]

    def made_by_pe(st):
        return st[0] in "TW" or st[0] == "D" and st[1:3] == (0, 0)

    t_use = number([st + (half,) for st in steps if made_by_pe(st) for half in range(1 if st[0] == "D" else 2)])
    l_use = number(kinds("MKQGL"))
    sg_use = number([st for st in steps if st[0] == "B" or st[0] == "A" and st[4] == 0])
    a_use = number([st[1:4] for st in steps if st[0] == "A" and st[4] == 0])
    e_use = number(kinds("L"))
    stage_use = number(kinds("KQL"))
    x_use, m_use, u_use, b_use = (number(kinds(c)) for c in "XMUB")
    res_use = number(dict.fromkeys(st[1:4] for st in kinds("B")))

    def half_before(b, h):
        return divmod(2 * b + h - 1, 2)

    def b_cols(st):
        return slice(0, H) if len(st) == 4 else slice(st[4] * H // 2, (st[4] + 1) * H // 2)

    def sg(kind, b, h, j):
        return sg_use[(kind, b, h, j) + ((0,) if kind == "A" else ())]

    x_v = data.rearrange("b (j p) k -> b j p k", p=P)
    out_v = out.rearrange("b (j p) n -> b j p n", p=P)
    w_v = weight.rearrange("(h n p) k -> h n p k", p=P, h=2)
    mask_v = mask.rearrange("(h n p) k -> h n p k", p=P, h=2)
    worg_v = w_org.rearrange("(h n p) i -> h p n i", p=P, h=2)
    down_v = down.rearrange("e i r -> i e r")
    up_v = up.rearrange("e r o -> (e r) o").rearrange("(t p) o -> p t o", p=P)
    bias_v = bias.rearrange("(o n) -> o n", o=1)
    dT_hi_dram = nc.dram_tensor("dT_hi_dram", [KC, P, 4, P], F32, kind="Internal").ap()
    dT_lo_dram = nc.dram_tensor("dT_lo_dram", [KC, P, 4, P], F32, kind="Internal").ap()

    ctx = ExitStack()
    with ctx:
        def sb(name, shape, dt=F32):
            return ctx.enter_context(nc.sbuf_tensor(name, shape, dt))

        def under(name, shape, dt=F32):
            with nc.sbuf_tensor(name, shape, dt) as t:
                return t

        def sem(name):
            return ctx.enter_context(nc.semaphore(name))

        ident = sb("ident", [P, P])
        blk_ones = sb("blk_ones", [P, P])
        ones = sb("ones", [P, P])
        bias_bc = sb("bias_bc", [P, H])
        xT_hi = sb("xT_hi", [P, NT, KC, P], F32R)
        xT_lo = sb("xT_lo", [P, NT, KC, P], F32R)
        wT_hi = sb("wT_hi", [P, KC, N], F32R)
        wT_lo = sb("wT_lo", [P, KC, N], F32R)
        up_hi = sb("up_hi", [P, 4, H], F32R)
        up_raw = under("up_raw", [P, 4, H])
        up_lo = sb("up_lo", [P, 4, H], F32R)
        dT_a = sb("dT_a", [P, 2, 2, 4, P], F32R)
        dT_b = under("dT_b", [P, 2, 2, 4, P], F32R)
        xin = sb("xin", [P, XIN, D])
        stage = sb("stage", [P, STG, H])
        res = sb("res", [P, RES, H])
        t_out = sb("t_out", [P, TRING, H])
        stats = sb("stats", [P, STAT, 2, 6])
        mv = sb("mv", [P, STAT, 2])
        nmean = sb("nmean", [P, STAT])
        rstd = sb("rstd", [P, STAT])
        neg_half = sb("neg_half", [P, 1])
        rowcnt = sb("rowcnt", [P, 2, N // BLK])
        bmask = sb("bmask", [P, 2, N // BLK])
        xpart = sb("xpart", [P, KC, NT])
        xsum = sb("xsum", [P, KC])
        keysT = sb("keysT", [P, E])
        kq = sb("kq", [P, E, KC])
        kqx = sb("kqx", [P, E, KC])
        kqs = sb("kqs", [P, E])
        nmax = sb("nmax", [P, 2])
        expo = sb("expo", [P, E])
        esum = sb("esum", [P, 2])
        coef = sb("coef", [P, 4])
        w_stage = under("w_stage", [P, 2 * WST, D])
        e = sb("e", [P, 2, KC, H], F32R)

        psT = ctx.enter_context(nc.psum_tensor("psT", [P, TR, H], F32))
        psL = ctx.enter_context(nc.psum_tensor("psL", [P, 2, H], F32))
        psSG = ctx.enter_context(nc.psum_tensor("psSG", [P, SGR, H], F32))

        xin_loaded = [sem(f"xin_loaded{i}") for i in range(XIN)]
        w_loaded = [sem(f"w_loaded{i}") for i in range(WST)]
        m_loaded = [sem(f"m_loaded{i}") for i in range(WST)]
        stage_loaded = [sem(f"stage_loaded{i}") for i in range(STG)]
        res_loaded = [sem(f"res_loaded{i}") for i in range(RES)]
        up_loaded = sem("up_loaded")
        down_loaded = [sem(f"down_loaded{i}") for i in range(4)]
        dT_loaded = [sem(f"dT_loaded{i}") for i in range(4)]
        dT_kept = [sem(f"dT_kept{i}") for i in range(2)]
        stored = [sem(f"stored{i}") for i in range(TRING)]
        bias_loaded = sem("bias_loaded")
        consts_zeroed = sem("consts_zeroed")
        consts_ready = sem("consts_ready")
        pe_T = sem("pe_T")
        pe_L = sem("pe_L")
        pe_SG = sem("pe_SG")
        act_T = sem("act_T")
        act_L = sem("act_L")
        act_exp = sem("act_exp")
        act_silu = sem("act_silu")
        act_U = sem("act_U")
        dve_T = sem("dve_T")
        dve_L = sem("dve_L")
        dve_w = sem("dve_w")
        dve_SG = sem("dve_SG")
        dve_U = sem("dve_U")
        dve_var = sem("dve_var")
        dve_cnt = sem("dve_cnt")
        dve_kq = sem("dve_kq")
        dve_max = sem("dve_max")
        dve_coef = sem("dve_coef")
        dve_own = sem("dve_own")
        pool_rstd = sem("pool_rstd")
        pool_xn = sem("pool_xn")
        pool_w = sem("pool_w")
        pool_out = sem("pool_out")

        block = ctx.enter_context(nc.Block())

        def stage_slot(st):
            return stage[:, stage_use[st] % STG, :]

        def wait_stage(eng, st):
            n = stage_use[st]
            eng.wait_ge(stage_loaded[n % STG], 16 * (n // STG + 1))

        place = {}
        loads_of = {}

        def put(key, ap, loaded):
            loads_of[loaded] = loads_of.get(loaded, 0) + 1
            place[key] = (ap, loaded, 16 * loads_of[loaded])

        for n in range(WST):
            put(("M", 0, n), w_stage[:, WST + n, :].bitcast(I32), m_loaded[n])
            put(("W", 0, n), w_stage[:, n, :], w_loaded[n])
        for j in range(NT):
            if 2 <= j < 6:
                put(("X", 0, j), w_stage[:, j - 2, :], w_loaded[j - 2])
            else:
                put(("X", 0, j), xin[:, j % 2, :], xin_loaded[j % 2])
        for n in range(4):
            put(("W", 1, n), xin[:, 0, :], xin_loaded[0])
            put(("M", 1, n), xin[:, 1, :].bitcast(I32), xin_loaded[1])
        for j in range(NT):
            put(("X", 1, j), xin[:, j % 2, :], xin_loaded[j % 2])

        def wait_place(eng, key):
            eng.wait_ge(place[key][1], place[key][2])

        def down_raw(k):
            return xin[:, k % 4 // 2, k % 2 * H:(k % 2 + 1) * H]

        def dT(st):
            k = st[3]
            slot = k % 2 if made_by_pe(st) else k % 4
            buf = dT_a if slot < 2 else dT_b
            return buf[:, slot % 2, 0], buf[:, slot % 2, 1]

        def masked_by_dve(h, n):
            return (h, n) == (0, 3)

        def wait_masked(eng, h, n):
            if masked_by_dve(h, n):
                eng.wait_ge(dve_w, 1)
            else:
                eng.wait_ge(pool_w, len([1 for _, g, m in m_use if (g, m) <= (h, n) and not masked_by_dve(g, m)]))

        def block_mask(w):
            return bmask[:, w % 2, :].rearrange("p (c o) -> p c o", o=1).to_broadcast([P, N // BLK, BLK])

        @block.sync
        def _(sp):
            by_stage = {n: st for st, n in stage_use.items()}

            def load_tile(key, src, before=None):
                if before:
                    before()
                sp.dma_start(place[key][0], src).then_inc(place[key][1], 16)

            def transposed(*key):
                return lambda: sp.wait_ge(pe_T, t_use[key + (0 if key[0] == "D" else 1,)] + 1)

            def counted(n):
                return lambda: sp.wait_ge(dve_cnt, m_use[("M", 1, n)] + 1)

            def load_x(b, j):
                if b == 0:
                    before = None if j < 2 else transposed("W", 0, j - 2) if j < 6 else transposed("T", 0, j - 6)
                elif j < 2:
                    before = lambda: sp.wait_ge(pe_L, l_use[("L", 0, 1, KC - 1)] + 1)
                else:
                    before = transposed("T", 1, j - 2)
                load_tile(("X", b, j), x_v[b, j], before)

            def load_small(st, dst, src):
                n = stage_use[st]
                if n >= STG:
                    sp.wait_ge(pe_L, l_use[by_stage[n - STG]] + 1)
                sp.dma_start(dst, src).then_inc(stage_loaded[n % STG], 16)

            def load(st):
                kind = st[0]
                if kind == "X":
                    load_x(st[1], st[2])
                elif kind == "R" and st[1] == 1:
                    n = st[2]
                    load_tile(("M", 1, n), mask_v[1, n], counted(n - 1) if n else transposed("D", 0, 0, 7))
                    load_tile(("W", 1, n), w_v[1, n], transposed("W", 1, n - 1) if n else transposed("D", 0, 0, 5))
                elif kind == "K":
                    load_small(st, stage_slot(st)[0:E, 0:QD], keys[:, :])
                elif kind == "Q":
                    load_small(st, stage_slot(st), wq[:, st[1] * H:(st[1] + 1) * H])
                elif kind == "U" and st[3] == 0:
                    _, b, h, _ = st
                    if (b, h) != (0, 0):
                        sp.wait_ge(pe_L, l_use[("L",) + half_before(b, h) + (KC - 1,)] + 1)
                    sp.dma_start(up_raw[:, :, :], up_v[:, :, h * H:(h + 1) * H]).then_inc(up_loaded, 16)
                elif kind == "D" and made_by_pe(st):
                    k = st[3]
                    if k < 4:
                        transposed("T", 0, 6 + k // 2)()
                    else:
                        transposed("D", 0, 0, k - 4)()
                    sp.dma_start(down_raw(k).rearrange("p (e r) -> p e r", e=E), down_v[k * P:(k + 1) * P])\
                      .then_inc(down_loaded[k % 4], 16)
                elif kind == "D":
                    _, b, h, k = st
                    if k >= 4:
                        sp.wait_ge(pe_L, l_use[("L", b, h, k - 4)] + 1)
                    else:
                        sp.wait_ge(pe_L, l_use[("L",) + half_before(b, h) + (KC - 1,)] + 1)
                        if k >= 2 and h:
                            transposed("W", 1, 3)()
                            sp.wait_ge(dve_cnt, m_use[("M", 1, 3)] + 1)
                        elif k >= 2:
                            transposed("T", 1, 7)()
                    if (b, h) == (0, 1):
                        sp.wait_ge(dT_kept[k % 2], 16 * 2 * 4)
                    for part, kept in enumerate((dT_hi_dram, dT_lo_dram)):
                        sp.dma_start(dT(st)[part].bitcast(F32), kept[k]).then_inc(dT_loaded[k % 4], 16)
                elif kind == "L":
                    _, b, h, k = st
                    load_small(st, stage_slot(st).rearrange("p (n i) -> p n i", n=4),
                               worg_v[h, :, :, k * P:(k + 1) * P])
                elif kind == "A" and st[3:] == (0, 0):
                    _, b, h, _, _ = st
                    q = 2 * b + h
                    if q:
                        sp.wait_ge(dve_SG, sg("A", (q - 1) // 2, (q - 1) % 2, NT - 1) + 1)
                    sp.dma_start(bias_bc[:, :], bias_v[:, h * H:(h + 1) * H].to_broadcast([P, H]))\
                      .then_inc(bias_loaded, 16)

            load(("X", 0, 0))
            for key in [("M", 0), ("W", 0), ("M", 1), ("M", 2), ("W", 1), ("M", 3), ("W", 2), ("W", 3)]:
                key = (key[0], 0, key[1])
                load_tile(key, (mask_v if key[0] == "M" else w_v)[0, key[2]])
            for st in steps:
                if st != ("X", 0, 0):
                    load(st)

        @block.tensor
        def _(pe):
            def product(ps, hi_l, lo_l, hi_r, lo_r, first, last):
                nc.tensor.matmul(ps, hi_l, hi_r, start=first, stop=False)
                nc.tensor.matmul(ps, hi_l, lo_r, start=False, stop=False)
                return nc.tensor.matmul(ps, lo_l, hi_r, start=False, stop=last)

            def transpose(ps, src, idn, first, last):
                return nc.tensor.matmul(ps, src, idn, start=first, stop=last, is_transpose=True)

            def take_T(n):
                if n >= TR:
                    pe.wait_ge(dve_T, n - TR + 1)
                return psT[:, n % TR, :]

            def take_L(n):
                if n >= 2:
                    pe.wait_ge(dve_L, n - 1)
                return psL[:, n % 2, :]

            def take_SG(n):
                if n >= SGR:
                    pe.wait_ge(dve_SG, n - SGR + 1)
                return psSG[:, n % SGR, :]

            def four_transposes(n, src):
                bank = take_T(n)
                for q in range(4):
                    ins = transpose(bank[:, q * P:(q + 1) * P], src(q), ident[:, :], True, True)
                ins.then_inc(pe_T, 1)

            pe.wait_ge(consts_ready, 3)
            for st in steps:
                if ("P",) + st in steps:
                    continue
                if st[0] == "P":
                    st = st[1:]
                kind = st[0]
                if kind in "TW":
                    if kind == "T":
                        src = place[("X",) + st[1:]][0]
                        pe.wait_ge(pool_xn, x_use[("X",) + st[1:]] + 1)
                    else:
                        src = place[st][0]
                        wait_masked(pe, st[1], st[2])
                    for half in range(2):
                        four_transposes(t_use[st + (half,)],
                                        lambda q: src[:, (4 * half + q) * P:(4 * half + q + 1) * P])
                elif kind == "M":
                    n, w = l_use[st], m_use[st]
                    bank = take_L(n)
                    pe.wait_ge(dve_cnt, w + 1)
                    nc.tensor.matmul(bank[:, 0:N // BLK], blk_ones[:, :], rowcnt[:, w % 2, :], start=True, stop=True)\
                        .then_inc(pe_L, 1)
                elif kind == "K":
                    n = l_use[st]
                    bank = take_L(n)
                    wait_stage(pe, st)
                    transpose(bank[:, 0:E], stage_slot(st)[0:E, 0:QD], ident[0:E, 0:E], True, True).then_inc(pe_L, 1)
                elif kind == "Q":
                    n = l_use[st]
                    bank = take_L(n)
                    wait_stage(pe, st)
                    pe.wait_ge(dve_L, l_use[("K",)] + 1)
                    for q in range(4):
                        ins = nc.tensor.matmul(bank[:, q * E:(q + 1) * E], stage_slot(st)[:, q * P:(q + 1) * P],
                                               keysT[:, :], start=True, stop=True)
                    ins.then_inc(pe_L, 1)
                elif kind == "A":
                    _, b, h, j, part = st
                    n = sg("A", b, h, j)
                    if part == 0:
                        take_SG(n)
                    pe.wait_ge(dve_T, t_use[("T", b, j, part)] + 1)
                    if b == 0 and j == 0:
                        pe.wait_ge(dve_T, t_use[("W", h, 3, part)] + 1)
                    bank = psSG[:, n % SGR, :]
                    for k in range(4 * part, 4 * part + 4):
                        ins = product(bank, xT_hi[:, j, k, :], xT_lo[:, j, k, :], wT_hi[:, k, h * H:(h + 1) * H],
                                      wT_lo[:, k, h * H:(h + 1) * H], k == 0, k == KC - 1)
                    if part == 1:
                        ins.then_inc(pe_SG, 1)
                elif kind == "B":
                    b, h, j = st[1:4]
                    n, cols = sg_use[st], b_cols(st)
                    bank = take_SG(n)[:, cols]
                    pe.wait_ge(dve_L, l_use[("L", b, h, KC - 1)] + 1)
                    for k in range(KC):
                        ins = product(bank, xT_hi[:, j, k, :], xT_lo[:, j, k, :], e[:, 0, k, cols], e[:, 1, k, cols],
                                      k == 0, k == KC - 1)
                    ins.then_inc(pe_SG, 1)
                elif kind == "G":
                    n = l_use[st]
                    bank = take_L(n)
                    pe.wait_ge(dve_kq, st[1] + 1)
                    nc.tensor.matmul(bank[:, 0:E], ones[:, :], kqs[:, :], start=True, stop=True).then_inc(pe_L, 1)
                elif kind == "D" and made_by_pe(st):
                    pe.wait_ge(down_loaded[st[3] % 4], 16 * (st[3] // 4 + 1))
                    four_transposes(t_use[st + (0,)], lambda q: down_raw(st[3])[:, q * P:(q + 1) * P])
                elif kind == "L":
                    _, b, h, k = st
                    n = l_use[st]
                    bank = take_L(n)
                    wait_stage(pe, st)
                    for q in range(4):
                        transpose(bank[:, q * P:(q + 1) * P], stage_slot(st)[:, q * P:(q + 1) * P], ident[:, :],
                                  q == 0, False)
                    d = ("D", b, h, k)
                    if made_by_pe(d):
                        pe.wait_ge(dve_T, t_use[d + (0,)] + 1)
                    else:
                        pe.wait_ge(dT_loaded[k % 4], 32 * (2 * (2 * b + h - 1) + k // 4 + 1))
                    hi, lo = dT(d)
                    for t in range(4):
                        if k == 0:
                            pe.wait_ge(dve_U, u_use[("U", b, h, t)] + 1)
                        ins = product(bank, hi[:, t, :], lo[:, t, :], up_hi[:, t, :], up_lo[:, t, :], False, t == 3)
                    ins.then_inc(pe_L, 1)

        def split_target(st, half):
            if st[0] == "T":
                ks = slice(4 * half, 4 * half + 4)
                return xT_hi[:, st[2], ks, :], xT_lo[:, st[2], ks, :]
            if st[0] == "W":
                ks, c = slice(4 * half, 4 * half + 4), (4 * st[1] + st[2]) * P
                return wT_hi[:, ks, c:c + P], wT_lo[:, ks, c:c + P]
            return dT(st)

        def psT_blocks(n):
            return psT[:, n % TR, :].rearrange("p (q c) -> p q c", q=4)

        @block.scalar
        def _(act):
            b_order = list(b_use)

            def load_res(i):
                b, h, j = list(res_use)[i]
                if i >= RES:
                    act.wait_ge(pool_out, i - RES + 1)
                act.dma_start(res[:, i % RES, :], x_v[b, j, :, h * H:(h + 1) * H]).then_inc(res_loaded[i % RES], 16)

            def keep(st):
                k = st[3]
                act.wait_ge(dve_T, t_use[st + (0,)] + 1)
                for part, kept in enumerate((dT_hi_dram, dT_lo_dram)):
                    act.dma_start(kept[k], dT(st)[part].bitcast(F32)).then_inc(dT_kept[k % 2], 16)

            def store(st):
                b, h, j = st[1:4]
                n, cols = a_use[(b, h, j)], b_cols(st)
                act.wait_ge(pool_out, b_use[st] + 1)
                act.dma_start(out_v[b, j, :, h * H + cols.start:h * H + cols.stop], t_out[:, n % TRING, cols])\
                   .then_inc(stored[n % TRING], 16)

            for st in steps:
                kind = st[0]
                if kind == "T":
                    _, b, j = st
                    if b == 1:
                        act.wait_ge(pe_SG, sg("B", 0, 1, j) + 1)
                        if j == 0:
                            act.wait_ge(dve_kq, 1)
                    for half in range(2):
                        n = t_use[st + (half,)]
                        act.wait_ge(pe_T, n + 1)
                        for q in range(4):
                            k = 4 * half + q
                            ins = nc.scalar.activation(xT_hi[:, j, k, :], psT[:, n % TR, q * P:(q + 1) * P], ACT.Copy,
                                                       accum_out=xpart[:, k, j:j + 1])
                        ins.then_inc(act_T, 1)
                elif kind == "W":
                    for half in range(2):
                        n = t_use[st + (half,)]
                        act.wait_ge(pe_T, n + 1)
                        nc.scalar.activation(split_target(st, half)[0], psT_blocks(n), ACT.Copy).then_inc(act_T, 1)
                elif kind == "D" and made_by_pe(st):
                    _, b, h, k = st
                    n = t_use[st + (0,)]
                    if k:
                        keep(("D", b, h, k - 1))
                    if k >= 2:
                        act.wait_ge(pe_L, l_use[("L", b, h, k - 2)] + 1)
                        act.wait_ge(dT_kept[k % 2], 32 * (k // 2))
                    act.wait_ge(pe_T, n + 1)
                    nc.scalar.activation(split_target(st, 0)[0], psT_blocks(n), ACT.Copy).then_inc(act_T, 1)
                elif kind == "U":
                    _, b, h, t = st
                    if t == 0:
                        act.wait_ge(dve_coef, b + 1)
                        if (b, h) != (0, 0):
                            act.wait_ge(pe_L, l_use[("L",) + half_before(b, h) + (KC - 1,)] + 1)
                        act.wait_ge(up_loaded, 16 * (2 * b + h + 1))
                    nc.scalar.activation(up_hi[:, t, :], up_raw[:, t, :], ACT.Copy, scale=coef[:, t:t + 1])\
                        .then_inc(act_U, 1)
                elif kind == "L":
                    _, b, h, k = st
                    n = l_use[st]
                    act.wait_ge(pe_L, n + 1)
                    nc.scalar.activation(e[:, 0, k, :], psL[:, n % 2, :], ACT.Copy).then_inc(act_L, 1)
                    if (b, h, k) == (0, 0, KC - 1):
                        keep(("D", 0, 0, KC - 1))
                    if (b, h, k) == (0, 0, 0):
                        for i in range(2):
                            load_res(i)
                elif kind == "G":
                    act.wait_ge(dve_max, st[1] + 1)
                    nc.scalar.activation(expo[:, :], psL[:, l_use[st] % 2, 0:E], ACT.Exp, bias=nmax[:, 1:2],
                                         scale=SCORE_SCALE, accum_out=esum[:, 0:1]).then_inc(act_exp, 1)
                elif kind == "B":
                    n, i = sg_use[st], b_use[st]
                    act.wait_ge(pe_SG, n + 1)
                    g = psSG[:, n % SGR, b_cols(st)]
                    nc.scalar.activation(g, g, ACT.Silu).then_inc(act_silu, 1)
                    if i:
                        store(b_order[i - 1])
                    if i + 2 < len(res_use):
                        load_res(i + 2)
            store(b_order[-1])
            for i in range(TRING):
                act.wait_ge(stored[i], 16 * len([st for st in b_order if a_use[st[1:4]] % TRING == i]))

        @block.vector
        def _(dve):
            own = [0]

            def mine(ins):
                own[0] += 1
                ins.then_inc(dve_own, 1)
                dve.wait_ge(dve_own, own[0])

            for st in steps:
                kind = st[0]
                if kind == "X":
                    n = x_use[st]
                    s, tile = n % STAT, place[st][0]
                    wait_place(dve, st)
                    for half in range(2):
                        ins = nc.vector.bn_stats(stats[:, s, half, :], tile[:, half * H:(half + 1) * H])
                    mine(ins)
                    mine(nc.vector.bn_aggr(mv[:, s, :], stats[:, s, :, :]))
                    if n >= STAT:
                        dve.wait_ge(pool_xn, n - STAT + 1)
                    nc.vector.tensor_scalar(nmean[:, s:s + 1], mv[:, s, 0:1], -1.0, None, ALU.mult)
                    nc.vector.tensor_scalar(rstd[:, s:s + 1], mv[:, s, 1:2], EPS, None, ALU.add).then_inc(dve_var, 1)
                elif kind in "TW" or kind == "D" and made_by_pe(st):
                    for half in range(1 if kind == "D" else 2):
                        n = t_use[st + (half,)]
                        hi, lo = split_target(st, half)
                        dve.wait_ge(act_T, n + 1)
                        nc.vector.tensor_tensor(lo, psT_blocks(n), hi.bitcast(F32), ALU.subtract).then_inc(dve_T, 1)
                elif kind == "R":
                    m = ("M",) + st[1:]
                    w = m_use[m]
                    wait_place(dve, m)
                    if w >= 2:
                        dve.wait_ge(pe_L, l_use[list(m_use)[w - 2]] + 1)
                    nc.vector.tensor_reduce(rowcnt[:, w % 2, :], place[m][0].rearrange("p (c k) -> p c k", k=BLK),
                                            AX.X, ALU.add).then_inc(dve_cnt, 1)
                elif kind == "N":
                    m = ("M",) + st[1:]
                    n, w = l_use[m], m_use[m]
                    if w >= 2:
                        wait_masked(dve, *list(m_use)[w - 2][1:])
                    dve.wait_ge(pe_L, n + 1)
                    nc.vector.tensor_scalar(bmask[:, w % 2, :], psL[:, n % 2, 0:N // BLK], 0.0, None, ALU.is_gt)\
                        .then_inc(dve_L, 1)
                elif kind == "V" and masked_by_dve(*st[1:]):
                    m, w = ("M",) + st[1:], ("W",) + st[1:]
                    tile = place[w][0].rearrange("p (c k) -> p c k", k=BLK)
                    wait_place(dve, w)
                    dve.wait_ge(dve_L, l_use[m] + 1)
                    nc.vector.tensor_tensor(tile, tile, block_mask(m_use[m]), ALU.mult).then_inc(dve_w, 1)
                elif kind == "K":
                    n = l_use[st]
                    dve.wait_ge(pe_L, n + 1)
                    nc.vector.tensor_copy(keysT[:, :], psL[:, n % 2, 0:E]).then_inc(dve_L, 1)
                elif kind == "Q":
                    n = l_use[st]
                    dve.wait_ge(pe_L, n + 1)
                    nc.vector.tensor_copy(kq[:, :, 4 * st[1]:4 * st[1] + 4].rearrange("p e q -> p q e"),
                                          psL[:, n % 2, 0:4 * E].rearrange("p (q e) -> p q e", q=4))\
                        .then_inc(dve_L, 1)
                elif kind == "C":
                    b = st[1]
                    if b:
                        dve.wait_ge(pe_L, l_use[("G", b - 1)] + 1)
                    dve.wait_ge(act_T, t_use[("T", b, NT - 1, 1)] + 1)
                    dve.wait_ge(dve_L, l_use[("Q", 1)] + 1)
                    mine(nc.vector.tensor_reduce(xsum[:, :], xpart[:, :, :], AX.X, ALU.add))
                    mine(nc.vector.tensor_tensor(kqx[:, :, :], kq[:, :, :],
                                                 xsum[:, :].rearrange("p (o k) -> p o k", o=1).to_broadcast([P, E, KC]),
                                                 ALU.mult))
                    nc.vector.tensor_reduce(kqs[:, :], kqx[:, :, :], AX.X, ALU.add).then_inc(dve_kq, 1)
                elif kind == "G":
                    b, n = st[1], l_use[st]
                    dve.wait_ge(pe_L, n + 1)
                    mine(nc.vector.tensor_reduce(nmax[:, 0:1], psL[:, n % 2, 0:E], AX.X, ALU.max))
                    nc.vector.tensor_scalar(nmax[:, 1:2], nmax[:, 0:1], -SCORE_SCALE, None, ALU.mult)\
                        .then_inc(dve_max, 1)
                    dve.wait_ge(act_exp, b + 1)
                    mine(nc.vector.reciprocal(esum[:, 1:2], esum[:, 0:1]))
                    if b:
                        dve.wait_ge(act_U, u_use[("U", b - 1, 1, 3)] + 1)
                    pairs = expo[:, :].rearrange("p (t two) -> p two t", two=2)
                    for half in range(2):
                        rows = slice(half * R, (half + 1) * R)
                        nc.vector.tensor_scalar(coef[rows, :], pairs[rows, half, :], esum[rows, 1:2], None, ALU.mult)\
                            .then_inc(dve_coef if half else dve_L, 1)
                elif kind == "U":
                    _, b, h, t = st
                    dve.wait_ge(act_U, u_use[st] + 1)
                    nc.vector.scalar_tensor_tensor(up_lo[:, t, :], up_raw[:, t, :], coef[:, t:t + 1],
                                                   up_hi[:, t, :].bitcast(F32), ALU.mult, ALU.subtract)\
                        .then_inc(dve_U, 1)
                elif kind == "L":
                    _, b, h, k = st
                    n = l_use[st]
                    dve.wait_ge(act_L, e_use[st] + 1)
                    nc.vector.tensor_tensor(e[:, 1, k, :], psL[:, n % 2, :], e[:, 0, k, :].bitcast(F32), ALU.subtract)\
                        .then_inc(dve_L, 1)
                elif kind == "A" and st[4] == 1:
                    _, b, h, j, _ = st
                    n, a = sg("A", b, h, j), a_use[(b, h, j)]
                    if j == 0:
                        dve.wait_ge(bias_loaded, 16 * (2 * b + h + 1))
                    if a >= TRING:
                        dve.wait_ge(stored[a % TRING], 16 * (a // TRING))
                    dve.wait_ge(pe_SG, n + 1)
                    nc.vector.tensor_tensor(t_out[:, a % TRING, :], psSG[:, n % SGR, :],
                                            bias_bc[:, :], ALU.add).then_inc(dve_SG, 1)
                elif kind == "B":
                    b, h, j = st[1:4]
                    n, a, cols = sg_use[st], a_use[(b, h, j)], b_cols(st)
                    dve.wait_ge(dve_SG, sg("A", b, h, j) + 1)
                    dve.wait_ge(act_silu, b_use[st] + 1)
                    t = t_out[:, a % TRING, cols]
                    nc.vector.tensor_tensor(t, t, psSG[:, n % SGR, cols], ALU.mult).then_inc(dve_SG, 1)

        @block.gpsimd
        def _(pool):
            nc.gpsimd.memset(neg_half[:, :], -0.5).then_inc(consts_zeroed, 1)
            nc.gpsimd.memset(ident[:, :], 0.0).then_inc(consts_zeroed, 1)
            nc.gpsimd.memset(blk_ones[:, :], 1.0).then_inc(consts_zeroed, 1)
            nc.gpsimd.memset(ones[:, :], 1.0).then_inc(consts_ready, 1)
            pool.wait_ge(consts_zeroed, 3)
            nc.gpsimd.affine_select(out=ident[:, :], in_=ident[:, :], compare_op=ALU.not_equal, fill=1.0,
                                    base=0, pattern=[[-1, P]], channel_multiplier=1).then_inc(consts_ready, 1)
            v = blk_ones[:, :].rearrange("p (g c) -> p g c", c=BLK)
            nc.gpsimd.affine_select(out=v, in_=v, compare_op=ALU.is_ge, fill=0.0, base=0,
                                    pattern=[[-BLK, P // BLK], [0, BLK]], channel_multiplier=1)\
                .then_inc(consts_zeroed, 1)
            pool.wait_ge(consts_zeroed, 4)
            nc.gpsimd.affine_select(out=v, in_=v, compare_op=ALU.is_ge, fill=0.0, base=BLK - 1,
                                    pattern=[[BLK, P // BLK], [0, BLK]], channel_multiplier=-1)\
                .then_inc(consts_ready, 1)
            for st in steps:
                kind = st[0]
                if kind == "X":
                    n = x_use[st]
                    s = n % STAT
                    pool.wait_ge(dve_var, n + 1)
                    nc.gpsimd.tensor_tensor(rstd[:, s:s + 1], rstd[:, s:s + 1], neg_half[:, :], ALU.pow)\
                        .then_inc(pool_rstd, 1)
                elif kind == "Y":
                    n = x_use[("X",) + st[1:]]
                    s, tile = n % STAT, place[("X",) + st[1:]][0]
                    pool.wait_ge(pool_rstd, n + 1)
                    nc.gpsimd.tensor_scalar(tile, tile, nmean[:, s:s + 1], rstd[:, s:s + 1], ALU.add, ALU.mult)\
                        .then_inc(pool_xn, 1)
                elif kind == "V" and not masked_by_dve(*st[1:]):
                    m, w = ("M",) + st[1:], ("W",) + st[1:]
                    tile = place[w][0].rearrange("p (c k) -> p c k", k=BLK)
                    wait_place(pool, w)
                    pool.wait_ge(dve_L, l_use[m] + 1)
                    nc.gpsimd.tensor_tensor(tile, tile, block_mask(m_use[m]), ALU.mult).then_inc(pool_w, 1)
                elif kind == "B":
                    a, i, cols = a_use[st[1:4]], res_use[st[1:4]], b_cols(st)
                    pool.wait_ge(res_loaded[i % RES], 16 * (i // RES + 1))
                    pool.wait_ge(dve_SG, sg_use[st] + 1)
                    t = t_out[:, a % TRING, cols]
                    nc.gpsimd.tensor_tensor(t, t, res[:, i % RES, cols], ALU.add).then_inc(pool_out, 1)


_INS = ["L0_attn_data", "L0_attn_mask", "L0_attn_weight", "L0_attn_bias", "L0_ffn_W_org", "L0_ffn_lora_down",
        "L0_ffn_lora_up", "L0_ffn_lora_keys", "L0_ffn_Wq"]


def kernel(**inputs):
    import numpy as _np
    import concourse.bacc as _bacc
    from concourse import mybir as _mybir
    from concourse.bass_utils import run_bass_kernel_spmd as _run

    nc = _bacc.Bacc("TRN2", target_bir_lowering=False, num_devices=1, dynamic_dma_scratch_size=1024)
    arrays, args = {}, []
    for name in _INS:
        a = _np.ascontiguousarray(inputs[name])
        arrays[f"in_{name}_dram"] = a
        args.append(nc.dram_tensor(f"in_{name}_dram", a.shape, _mybir.dt.from_np(a.dtype), kind="ExternalInput").ap())
    shape = inputs["L0_attn_data"].shape
    args.append(nc.dram_tensor("out_dram", shape, F32, kind="ExternalOutput").ap())
    gated_block_linear_lora(nc, *args)
    r = _run(nc, [arrays], core_ids=[0])
    return r.results[0]["out_dram"]
```

```python
from contextlib import ExitStack

import concourse.bass as bass
from concourse import mybir

P = 128
H = 512
F32 = mybir.dt.float32
F32R = mybir.dt.float32r
I32 = mybir.dt.int32
ALU = mybir.AluOpType
ACT = mybir.ActivationFunctionType
AX = mybir.AxisListType

XIN = 2
WST = 4
STAT = 4
STG = 4
RES = 2
TRING = 6
WORK = 6
SGR = 2
BLK = 32


def schedule():
    def A(b, h, j):
        return [("A", b, h, j, 0), ("A", b, h, j, 1)]

    def up_and_first_down(b, h):
        return [("D", b, h, 0)] + [("U", b, h, t) for t in range(4)]

    def make_E(b, h):
        s = []
        for k in range(8):
            if k < 7:
                s.append(("D", b, h, k + 1))
            if b == 0:
                s.append(("O", h, k))
            s.append(("L", b, h, k))
        return s

    s = [("X", 0, 0), ("Y", 0, 0), ("R", 0, 0), ("M", 0, 0), ("N", 0, 0), ("V", 0, 0), ("P", "T", 0, 0),
         ("R", 0, 1), ("M", 0, 1), ("N", 0, 1), ("V", 0, 1), ("T", 0, 0), ("P", "W", 0, 0),
         ("R", 0, 2), ("M", 0, 2), ("W", 0, 0), ("N", 0, 2), ("V", 0, 2), ("W", 0, 1), ("P", "W", 0, 2)]
    s += [("A", 0, 0, 0, 0, 0), ("X", 0, 1), ("Y", 0, 1), ("R", 0, 3), ("W", 0, 2), ("M", 0, 3), ("N", 0, 3),
          ("V", 0, 3), ("P", "T", 0, 1), ("A", 0, 0, 0, 1, 0), ("T", 0, 1), ("W", 0, 3), ("X", 0, 2), ("Y", 0, 2)]
    parts = [("A", 0, 0, j, p, c) for j, c in ((1, 0), (0, 1), (1, 1)) for p in range(2)]
    parts += [st for j in range(2, 6) for st in A(0, 0, j)]
    s += [parts.pop(0), ("X", 0, 3), ("Y", 0, 3), parts.pop(0), parts.pop(0), ("X", 0, 4), ("Y", 0, 4), parts.pop(0)]
    for j in range(2, 8):
        s += [parts.pop(0), ("T", 0, j)]
        s += [("X", 0, j + 3), ("Y", 0, j + 3)] if j + 3 < 8 else []
        s += {3: [("K",)], 5: [("Q", 0)], 6: [("Q", 1)]}.get(j, [])
    s += [parts.pop(0), ("C", 0), parts.pop(0), ("G", 0)] + up_and_first_down(0, 0) + [parts.pop(0)]
    s += make_E(0, 0)
    groups = [parts, [("B", 0, 0, 0)], [("B", 0, 0, 1)], A(0, 0, 6), [("B", 0, 0, 2)], A(0, 0, 7),
              [("B", 0, 0, 3)], [("B", 0, 0, 4)], [("B", 0, 0, 5)], [("B", 0, 0, 6)]]
    s.append(("R", 1, 0))
    for i, group in enumerate(groups):
        n = (i - 1) // 2
        s += group
        if i % 2:
            s += [("M", 1, n), ("N", 1, n), ("V", 1, n)] if n < 4 else []
        elif i:
            s += [("W", 1, n)] + ([("R", 1, n + 1)] if n < 3 else [])
    for b in range(2):
        if b:
            s += A(1, 0, 0) + [("C", 1)] + A(1, 0, 1) + [("G", 1)] + A(1, 0, 2) + up_and_first_down(1, 0)
            s += A(1, 0, 3)
            s += make_E(1, 0) + A(1, 0, 4) + [("B", 1, 0, 0), ("B", 1, 0, 1)]
            for j in range(5, 8):
                s += A(1, 0, j) + [("B", 1, 0, j - 3)]
            s += [("B", 1, 0, 5), ("B", 1, 0, 6)]
        s += up_and_first_down(b, 1) + [("B", b, 0, 7)] + make_E(b, 1) + A(b, 1, 0)
        if b == 0:
            s += [("X", 1, 0), ("Y", 1, 0)]
        for j in range(8):
            s += A(b, 1, j + 1) if j < 7 else []
            s += [("B", b, 1, j)] if (b, j) != (1, 7) else [("B", 1, 1, 7, 0), ("B", 1, 1, 7, 1)]
            if b == 0:
                s += [("X", 1, j + 1), ("Y", 1, j + 1)] if j < 7 else []
                s.append(("T", 1, j))
    return s


def gated_block_linear_lora(nc, data, mask, weight, bias, w_org, down, up, keys, wq, out):
    NB, S, D = data.shape
    N = weight.shape[0]
    E, _, R = down.shape
    QD = keys.shape[1]
    NT, KC = S // P, D // P
    assert (NB, NT, KC, N, E * R, QD) == (2, 8, 8, 2 * H, H, P)
    EPS = 1e-5
    SCORE_SCALE = 1.0 / (S * float(QD) ** 0.5)

    steps = schedule()

    def number(keys):
        return {key: n for n, key in enumerate(keys)}

    def kinds(letters):
        return [st for st in steps if st[0] in letters]

    def made_by_pe(st):
        return st[0] in "TWO" or st[0] == "D" and st[1:3] == (0, 0)

    t_use = number([st + (half,) for st in steps if made_by_pe(st) for half in range(1 if st[0] in "DO" else 2)])
    l_use = number(kinds("MKQGL"))
    pe_order = [st[1:] if st[0] == "P" else st for st in steps if ("P",) + st not in steps]
    work_order = [(ring, ring_use[key]) for st in pe_order
                  for ring, ring_use in (("T", t_use), ("L", l_use))
                  for key in (st, st + (0,), st + (1,)) if key in ring_use]
    work_use = number(work_order)
    sg_use = number(dict.fromkeys(st if st[0] == "B" else st[:4] for st in kinds("AB")))
    a_use = number(dict.fromkeys(st[1:4] for st in kinds("A")))
    e_use = number(kinds("L"))
    stage_use = number([st for st in steps if st[0] in "KQO" or st[0] == "L" and st[1] == 1])
    x_use, m_use, u_use, b_use = (number(kinds(c)) for c in "XMUB")
    res_use = number(dict.fromkeys(st[1:4] for st in kinds("B")))

    def half_before(b, h):
        return divmod(2 * b + h - 1, 2)

    def b_cols(st):
        return slice(0, H) if len(st) == 4 else slice(st[4] * H // 2, (st[4] + 1) * H // 2)

    def a_part(st):
        part, c = st[4], st[5:]
        cols = slice(c[0] * H // 2, (c[0] + 1) * H // 2) if c else slice(0, H)
        return cols, part == 0 and c in ((), (0,)), part == 1 and c in ((), (1,))

    x_v = data.rearrange("b (j p) k -> b j p k", p=P)
    out_v = out.rearrange("b (j p) n -> b j p n", p=P)
    w_v = weight.rearrange("(h n p) k -> h n p k", p=P, h=2)
    mask_v = mask.rearrange("(h n p) k -> h n p k", p=P, h=2)
    worg_v = w_org.rearrange("(h n p) i -> h p n i", p=P, h=2)
    down_v = down.rearrange("e i r -> i e r")
    up_v = up.rearrange("e r o -> (e r) o").rearrange("(t p) o -> p t o", p=P)
    bias_v = bias.rearrange("(o n) -> o n", o=1)
    dT_hi_dram = nc.dram_tensor("dT_hi_dram", [KC, P, 4, P], F32, kind="Internal").ap()
    dT_lo_dram = nc.dram_tensor("dT_lo_dram", [KC, P, 4, P], F32, kind="Internal").ap()

    worgT_dram = nc.dram_tensor("worgT_dram", [2, KC, P, H], F32, kind="Internal").ap()

    ctx = ExitStack()
    with ctx:
        def sb(name, shape, dt=F32):
            return ctx.enter_context(nc.sbuf_tensor(name, shape, dt))

        def under(name, shape, dt=F32):
            with nc.sbuf_tensor(name, shape, dt) as t:
                return t

        def sem(name):
            return ctx.enter_context(nc.semaphore(name))

        ident = sb("ident", [P, P])
        blk_ones = sb("blk_ones", [P, P])
        ones = sb("ones", [P, P])
        bias_bc = sb("bias_bc", [P, H])
        xT_hi = sb("xT_hi", [P, NT, KC, P], F32R)
        xT_lo = sb("xT_lo", [P, NT, KC, P], F32R)
        wT_hi = sb("wT_hi", [P, KC, N], F32R)
        wT_lo = sb("wT_lo", [P, KC, N], F32R)
        up_hi = sb("up_hi", [P, 4, H], F32R)
        up_raw = under("up_raw", [P, 4, H])
        up_lo = sb("up_lo", [P, 4, H], F32R)
        dT_a = sb("dT_a", [P, 2, 2, 4, P], F32R)
        dT_b = under("dT_b", [P, 2, 2, 4, P], F32R)
        xin = sb("xin", [P, XIN, D])
        stage = sb("stage", [P, STG, H])
        res = sb("res", [P, RES, H])
        t_out = sb("t_out", [P, TRING, H])
        stats = sb("stats", [P, STAT, 2, 6])
        mv = sb("mv", [P, STAT, 2])
        nmean = sb("nmean", [P, STAT])
        rstd = sb("rstd", [P, STAT])
        neg_half = sb("neg_half", [P, 1])
        rowcnt = sb("rowcnt", [P, 2, N // BLK])
        bmask = sb("bmask", [P, 2, N // BLK])
        xpart = sb("xpart", [P, KC, NT])
        xsum = sb("xsum", [P, KC])
        keysT = sb("keysT", [P, E])
        kq = sb("kq", [P, E, KC])
        kqx = sb("kqx", [P, E, KC])
        kqs = sb("kqs", [P, E])
        nmax = sb("nmax", [P, 2])
        expo = sb("expo", [P, E])
        esum = sb("esum", [P, 2])
        coef = sb("coef", [P, 4])
        w_stage = under("w_stage", [P, 2 * WST, D])
        e = sb("e", [P, 2, KC, H], F32R)

        psW = ctx.enter_context(nc.psum_tensor("psW", [P, WORK, H], F32))
        psSG = ctx.enter_context(nc.psum_tensor("psSG", [P, SGR, H], F32))

        xin_loaded = [sem(f"xin_loaded{i}") for i in range(XIN)]
        w_loaded = [sem(f"w_loaded{i}") for i in range(WST)]
        m_loaded = [sem(f"m_loaded{i}") for i in range(WST)]
        stage_loaded = [sem(f"stage_loaded{i}") for i in range(STG)]
        res_loaded = [sem(f"res_loaded{i}") for i in range(RES)]
        up_loaded = sem("up_loaded")
        down_loaded = [sem(f"down_loaded{i}") for i in range(4)]
        dT_loaded = [sem(f"dT_loaded{i}") for i in range(4)]
        dT_kept = [sem(f"dT_kept{i}") for i in range(2)]
        stored = [sem(f"stored{i}") for i in range(TRING)]
        bias_loaded = sem("bias_loaded")
        consts_zeroed = sem("consts_zeroed")
        consts_ready = sem("consts_ready")
        stage_kept = [sem(f"stage_kept{i}") for i in range(STG)]
        pe_T = sem("pe_T")
        pe_L = sem("pe_L")
        pe_SG = sem("pe_SG")
        act_T = sem("act_T")
        act_L = sem("act_L")
        act_exp = sem("act_exp")
        act_silu = sem("act_silu")
        act_U = sem("act_U")
        dve_T = sem("dve_T")
        dve_L = sem("dve_L")
        dve_sum = sem("dve_sum")
        dve_w = sem("dve_w")
        dve_SG = sem("dve_SG")
        dve_U = sem("dve_U")
        dve_var = sem("dve_var")
        dve_cnt = sem("dve_cnt")
        dve_kq = sem("dve_kq")
        dve_max = sem("dve_max")
        dve_coef = sem("dve_coef")
        dve_own = sem("dve_own")
        pool_rstd = sem("pool_rstd")
        pool_xn = sem("pool_xn")
        pool_w = sem("pool_w")
        pool_out = sem("pool_out")
        dve_out = sem("dve_out")

        block = ctx.enter_context(nc.Block())

        def stage_slot(st):
            return stage[:, stage_use[st] % STG, :]

        def wait_stage(eng, st):
            n = stage_use[st]
            eng.wait_ge(stage_loaded[n % STG], 16 * (n // STG + 1))

        def bank_T(n):
            return psW[:, work_use[("T", n)] % WORK, :]

        def blocks_T(n):
            return bank_T(n).rearrange("p (q c) -> p q c", q=4)

        def bank_L(n):
            return psW[:, work_use[("L", n)] % WORK, :]

        worg_t_uses = [n for st, n in t_use.items() if st[0] == "O"]

        place = {}
        loads_of = {}

        def put(key, ap, loaded):
            loads_of[loaded] = loads_of.get(loaded, 0) + 1
            place[key] = (ap, loaded, 16 * loads_of[loaded])

        for n in range(WST):
            put(("M", 0, n), w_stage[:, WST + n, :].bitcast(I32), m_loaded[n])
            put(("W", 0, n), w_stage[:, n, :], w_loaded[n])
        for j in range(NT):
            if 2 <= j < 6:
                put(("X", 0, j), w_stage[:, j - 2, :], w_loaded[j - 2])
            elif j >= 6:
                put(("X", 0, j), w_stage[:, WST + j - 6, :], m_loaded[j - 6])
            else:
                put(("X", 0, j), xin[:, j % 2, :], xin_loaded[j % 2])
        for n in range(4):
            put(("W", 1, n), xin[:, 0, :], xin_loaded[0])
            put(("M", 1, n), xin[:, 1, :].bitcast(I32), xin_loaded[1])
        for j in range(NT):
            put(("X", 1, j), xin[:, j % 2, :], xin_loaded[j % 2])

        def wait_place(eng, key):
            eng.wait_ge(place[key][1], place[key][2])

        def down_raw(k):
            return xin[:, k % 4 // 2, k % 2 * H:(k % 2 + 1) * H]

        def dT(st):
            k = st[3]
            slot = k % 2 if made_by_pe(st) else k % 4
            buf = dT_a if slot < 2 else dT_b
            return buf[:, slot % 2, 0], buf[:, slot % 2, 1]

        def wait_read(eng, n):
            if n in worg_t_uses:
                eng.wait_ge(act_T, n + 1)
            else:
                eng.wait_ge(dve_T, n + 1 - len([m for m in worg_t_uses if m < n]))

        def masked_by_dve(h, n):
            return (h, n) == (0, 3)

        def wait_masked(eng, h, n):
            if masked_by_dve(h, n):
                eng.wait_ge(dve_w, 1)
            else:
                eng.wait_ge(pool_w, len([1 for _, g, m in m_use if (g, m) <= (h, n) and not masked_by_dve(g, m)]))

        last_b = steps[-1]

        def wait_out(eng, st):
            if st == last_b:
                eng.wait_ge(dve_out, 1)
            else:
                eng.wait_ge(pool_out, b_use[st] + 1)

        def block_mask(w):
            return bmask[:, w % 2, :].rearrange("p (c o) -> p c o", o=1).to_broadcast([P, N // BLK, BLK])

        @block.sync
        def _(sp):
            by_stage = {n: st for st, n in stage_use.items()}

            def load_tile(key, src, before=None):
                if before:
                    before()
                sp.dma_start(place[key][0], src).then_inc(place[key][1], 16)

            def transposed(*key):
                return lambda: sp.wait_ge(pe_T, t_use[key + (0 if key[0] == "D" else 1,)] + 1)

            def counted(h, n):
                return lambda: sp.wait_ge(dve_cnt, m_use[("M", h, n)] + 1)

            def load_x(b, j):
                if b == 0:
                    before = transposed("W", 0, j - 2) if j < 6 else counted(0, j - 6)
                elif j < 2:
                    before = lambda: sp.wait_ge(pe_L, l_use[("L", 0, 1, KC - 1)] + 1)
                else:
                    before = transposed("T", 1, j - 2)
                load_tile(("X", b, j), x_v[b, j], before)

            def keeps(n):
                return 16 * len([m for st, m in stage_use.items() if st[0] == "O" and m <= n and m % STG == n % STG])

            def load_small(st, dst, src):
                n = stage_use[st]
                if n >= STG:
                    last = by_stage[n - STG]
                    if last[0] in "KQ":
                        sp.wait_ge(pe_L, l_use[last] + 1)
                    else:
                        sp.wait_ge(dve_sum, e_use[last if last[0] == "L" else ("L", 0) + last[1:]] + 1)
                    if last[0] == "O":
                        sp.wait_ge(stage_kept[n % STG], keeps(n - STG))
                sp.dma_start(dst, src).then_inc(stage_loaded[n % STG], 16)

            def load(st):
                kind = st[0]
                if kind == "X":
                    load_x(st[1], st[2])
                elif kind == "R" and st[1] == 1:
                    n = st[2]
                    load_tile(("M", 1, n), mask_v[1, n], counted(1, n - 1) if n else transposed("D", 0, 0, 7))
                    load_tile(("W", 1, n), w_v[1, n], transposed("W", 1, n - 1) if n else transposed("D", 0, 0, 5))
                elif kind == "K":
                    load_small(st, stage_slot(st)[0:E, 0:QD], keys[:, :])
                elif kind == "Q":
                    load_small(st, stage_slot(st), wq[:, st[1] * H:(st[1] + 1) * H])
                elif kind == "U" and st[3] == 0:
                    _, b, h, _ = st
                    if (b, h) != (0, 0):
                        sp.wait_ge(pe_L, l_use[("L",) + half_before(b, h) + (KC - 1,)] + 1)
                    sp.dma_start(up_raw[:, :, :], up_v[:, :, h * H:(h + 1) * H]).then_inc(up_loaded, 16)
                elif kind == "D" and made_by_pe(st):
                    if st[3] >= 4:
                        load_down(st[3], transposed("D", 0, 0, st[3] - 4))
                elif kind == "D":
                    _, b, h, k = st
                    if k >= 4:
                        sp.wait_ge(pe_L, l_use[("L", b, h, k - 4)] + 1)
                    else:
                        sp.wait_ge(pe_L, l_use[("L",) + half_before(b, h) + (KC - 1,)] + 1)
                        if k >= 2 and h:
                            transposed("W", 1, 3)()
                            sp.wait_ge(dve_cnt, m_use[("M", 1, 3)] + 1)
                        elif k >= 2:
                            transposed("T", 1, 7)()
                    if (b, h) == (0, 1):
                        sp.wait_ge(dT_kept[k % 2], 16 * 2 * 4)
                    for part, kept in enumerate((dT_hi_dram, dT_lo_dram)):
                        sp.dma_start(dT(st)[part].bitcast(F32), kept[k]).then_inc(dT_loaded[k % 4], 16)
                elif kind == "O":
                    _, h, k = st
                    load_small(st, stage_slot(st).rearrange("p (n i) -> p n i", n=4),
                               worg_v[h, :, :, k * P:(k + 1) * P])
                elif kind == "L" and st[1] == 1:
                    _, b, h, k = st
                    if (h, k) == (0, 0):
                        for i in range(STG):
                            sp.wait_ge(stage_kept[i], keeps(max(m for m in stage_use.values() if m % STG == i)))
                    load_small(st, stage_slot(st), worgT_dram[h, k])
                elif kind == "A" and st[3] == 0 and a_part(st)[1]:
                    b, h = st[1:3]
                    q = 2 * b + h
                    if q:
                        sp.wait_ge(dve_SG, sg_use[("A",) + half_before(b, h) + (NT - 1,)] + 1)
                    sp.dma_start(bias_bc[:, :], bias_v[:, h * H:(h + 1) * H].to_broadcast([P, H]))\
                      .then_inc(bias_loaded, 16)

            def load_down(k, before):
                before()
                sp.dma_start(down_raw(k).rearrange("p (e r) -> p e r", e=E), down_v[k * P:(k + 1) * P])\
                  .then_inc(down_loaded[k % 4], 16)

            for name, n in [("X", 0), ("M", 0), ("W", 0), ("M", 1), ("W", 1), ("M", 2), ("X", 1), ("W", 2),
                            ("M", 3), ("W", 3)]:
                load_tile((name, 0, n), {"X": x_v, "M": mask_v, "W": w_v}[name][0, n])
            for st in steps:
                if st not in (("X", 0, 0), ("X", 0, 1)):
                    load(st)
                if st == ("X", 0, NT - 1):
                    for k in range(4):
                        load_down(k, transposed("T", 0, k // 2))

        @block.tensor
        def _(pe):
            def product(ps, hi_l, lo_l, hi_r, lo_r, first, last):
                nc.tensor.matmul(ps, hi_l, hi_r, start=first, stop=False)
                nc.tensor.matmul(ps, hi_l, lo_r, start=False, stop=False)
                return nc.tensor.matmul(ps, lo_l, hi_r, start=False, stop=last)

            def transpose(ps, src, idn):
                return nc.tensor.matmul(ps, src, idn, start=True, stop=True, is_transpose=True)

            def take_work(ring, n):
                w = work_use[(ring, n)]
                if w >= WORK:
                    ring_before, n_before = work_order[w - WORK]
                    if ring_before == "T":
                        wait_read(pe, n_before)
                    else:
                        pe.wait_ge(dve_L, n_before + 1)
                return psW[:, w % WORK, :]

            def take_SG(n):
                if n >= SGR:
                    pe.wait_ge(dve_SG, n - SGR + 1)
                return psSG[:, n % SGR, :]

            def four_transposes(n, src):
                bank = take_work("T", n)
                for q in range(4):
                    ins = transpose(bank[:, q * P:(q + 1) * P], src(q), ident[:, :])
                ins.then_inc(pe_T, 1)

            pe.wait_ge(consts_ready, 3)
            for st in pe_order:
                kind = st[0]
                if kind in "TW":
                    if kind == "T":
                        src = place[("X",) + st[1:]][0]
                        pe.wait_ge(pool_xn, x_use[("X",) + st[1:]] + 1)
                    else:
                        src = place[st][0]
                        wait_masked(pe, st[1], st[2])
                    for half in range(2):
                        four_transposes(t_use[st + (half,)],
                                        lambda q: src[:, (4 * half + q) * P:(4 * half + q + 1) * P])
                elif kind == "M":
                    n, w = l_use[st], m_use[st]
                    bank = take_work("L", n)
                    pe.wait_ge(dve_cnt, w + 1)
                    nc.tensor.matmul(bank[:, 0:N // BLK], blk_ones[:, :], rowcnt[:, w % 2, :], start=True, stop=True)\
                        .then_inc(pe_L, 1)
                elif kind == "K":
                    n = l_use[st]
                    bank = take_work("L", n)
                    wait_stage(pe, st)
                    transpose(bank[:, 0:E], stage_slot(st)[0:E, 0:QD], ident[0:E, 0:E]).then_inc(pe_L, 1)
                elif kind == "Q":
                    n = l_use[st]
                    bank = take_work("L", n)
                    wait_stage(pe, st)
                    pe.wait_ge(dve_L, l_use[("K",)] + 1)
                    for q in range(4):
                        ins = nc.tensor.matmul(bank[:, q * E:(q + 1) * E], stage_slot(st)[:, q * P:(q + 1) * P],
                                               keysT[:, :], start=True, stop=True)
                    ins.then_inc(pe_L, 1)
                elif kind == "A":
                    b, h, j, part = st[1:5]
                    cols, first, last = a_part(st)
                    n = sg_use[("A", b, h, j)]
                    if first:
                        take_SG(n)
                    wait_read(pe, t_use[("T", b, j, part)])
                    if b == 0 and cols != slice(0, H):
                        wait_read(pe, t_use[("W", h, cols.stop // P - 1, part)])
                    elif b == 0 and j == 0:
                        wait_read(pe, t_use[("W", h, 3, part)])
                    bank = psSG[:, n % SGR, cols]
                    w_cols = slice(h * H + cols.start, h * H + cols.stop)
                    for k in range(4 * part, 4 * part + 4):
                        ins = product(bank, xT_hi[:, j, k, :], xT_lo[:, j, k, :], wT_hi[:, k, w_cols],
                                      wT_lo[:, k, w_cols], k == 0, k == KC - 1)
                    if last:
                        ins.then_inc(pe_SG, 1)
                elif kind == "B":
                    b, h, j = st[1:4]
                    n, cols = sg_use[st], b_cols(st)
                    bank = take_SG(n)[:, cols]
                    for k in range(KC):
                        if j == 0:
                            pe.wait_ge(dve_L, l_use[("L", b, h, k)] + 1)
                        ins = product(bank, xT_hi[:, j, k, :], xT_lo[:, j, k, :], e[:, 0, k, cols], e[:, 1, k, cols],
                                      k == 0, k == KC - 1)
                    ins.then_inc(pe_SG, 1)
                elif kind == "G":
                    n = l_use[st]
                    bank = take_work("L", n)
                    pe.wait_ge(dve_kq, st[1] + 1)
                    nc.tensor.matmul(bank[:, 0:E], ones[:, :], kqs[:, :], start=True, stop=True).then_inc(pe_L, 1)
                elif kind == "D" and made_by_pe(st):
                    pe.wait_ge(down_loaded[st[3] % 4], 16 * (st[3] // 4 + 1))
                    four_transposes(t_use[st + (0,)], lambda q: down_raw(st[3])[:, q * P:(q + 1) * P])
                elif kind == "O":
                    wait_stage(pe, st)
                    four_transposes(t_use[st + (0,)], lambda q: stage_slot(st)[:, q * P:(q + 1) * P])
                elif kind == "L":
                    _, b, h, k = st
                    n = l_use[st]
                    bank = take_work("L", n)
                    d = ("D", b, h, k)
                    if made_by_pe(d):
                        wait_read(pe, t_use[d + (0,)])
                    else:
                        pe.wait_ge(dT_loaded[k % 4], 32 * (2 * (2 * b + h - 1) + k // 4 + 1))
                    hi, lo = dT(d)
                    for t in range(4):
                        if k == 0:
                            pe.wait_ge(dve_U, u_use[("U", b, h, t)] + 1)
                        ins = product(bank, hi[:, t, :], lo[:, t, :], up_hi[:, t, :], up_lo[:, t, :], t == 0, t == 3)
                    ins.then_inc(pe_L, 1)

        def split_target(st, half):
            if st[0] == "T":
                ks = slice(4 * half, 4 * half + 4)
                return xT_hi[:, st[2], ks, :], xT_lo[:, st[2], ks, :]
            if st[0] == "W":
                ks, c = slice(4 * half, 4 * half + 4), (4 * st[1] + st[2]) * P
                return wT_hi[:, ks, c:c + P], wT_lo[:, ks, c:c + P]
            return dT(st)


        @block.scalar
        def _(act):
            b_order = list(b_use)

            def load_res(i):
                b, h, j = list(res_use)[i]
                if i >= RES:
                    act.wait_ge(pool_out, i - RES + 1)
                act.dma_start(res[:, i % RES, :], x_v[b, j, :, h * H:(h + 1) * H]).then_inc(res_loaded[i % RES], 16)

            def keep(st):
                k = st[3]
                wait_read(act, t_use[st + (0,)])
                for part, kept in enumerate((dT_hi_dram, dT_lo_dram)):
                    act.dma_start(kept[k], dT(st)[part].bitcast(F32)).then_inc(dT_kept[k % 2], 16)

            def store(st):
                b, h, j = st[1:4]
                n, cols = a_use[(b, h, j)], b_cols(st)
                wait_out(act, st)
                act.dma_start(out_v[b, j, :, h * H + cols.start:h * H + cols.stop], t_out[:, n % TRING, cols])\
                   .then_inc(stored[n % TRING], 16)

            for st in steps:
                kind = st[0]
                if kind == "T":
                    _, b, j = st
                    if b == 1:
                        act.wait_ge(pe_SG, sg_use[("B", 0, 1, j)] + 1)
                        if j == 0:
                            act.wait_ge(dve_kq, 1)
                    for half in range(2):
                        n = t_use[st + (half,)]
                        act.wait_ge(pe_T, n + 1)
                        for q in range(4):
                            k = 4 * half + q
                            ins = nc.scalar.activation(xT_hi[:, j, k, :], bank_T(n)[:, q * P:(q + 1) * P], ACT.Copy,
                                                       accum_out=xpart[:, k, j:j + 1])
                        ins.then_inc(act_T, 1)
                elif kind == "W":
                    for half in range(2):
                        n = t_use[st + (half,)]
                        act.wait_ge(pe_T, n + 1)
                        nc.scalar.activation(split_target(st, half)[0], blocks_T(n), ACT.Copy).then_inc(act_T, 1)
                elif kind == "D" and made_by_pe(st):
                    _, b, h, k = st
                    n = t_use[st + (0,)]
                    if k:
                        keep(("D", b, h, k - 1))
                    if k >= 2:
                        act.wait_ge(pe_L, l_use[("L", b, h, k - 2)] + 1)
                        act.wait_ge(dT_kept[k % 2], 32 * (k // 2))
                    act.wait_ge(pe_T, n + 1)
                    nc.scalar.activation(split_target(st, 0)[0], blocks_T(n), ACT.Copy).then_inc(act_T, 1)
                elif kind == "U":
                    _, b, h, t = st
                    if t == 0:
                        act.wait_ge(dve_coef, b + 1)
                        if (b, h) != (0, 0):
                            act.wait_ge(pe_L, l_use[("L",) + half_before(b, h) + (KC - 1,)] + 1)
                        act.wait_ge(up_loaded, 16 * (2 * b + h + 1))
                    nc.scalar.activation(up_hi[:, t, :], up_raw[:, t, :], ACT.Copy, scale=coef[:, t:t + 1])\
                        .then_inc(act_U, 1)
                elif kind == "O":
                    _, h, k = st
                    n = t_use[st + (0,)]
                    act.wait_ge(pe_T, n + 1)
                    nc.scalar.activation(stage_slot(st), bank_T(n), ACT.Copy).then_inc(act_T, 1)
                    act.wait_ge(act_T, n + 1)
                    act.dma_start(worgT_dram[h, k], stage_slot(st)).then_inc(stage_kept[stage_use[st] % STG], 16)
                elif kind == "L":
                    _, b, h, k = st
                    n = l_use[st]
                    act.wait_ge(dve_sum, e_use[st] + 1)
                    nc.scalar.activation(e[:, 0, k, :], bank_L(n), ACT.Copy).then_inc(act_L, 1)
                    if (b, h, k) == (0, 0, KC - 1):
                        keep(("D", 0, 0, KC - 1))
                    if (b, h, k) == (0, 0, KC - 2):
                        load_res(0)
                elif kind == "G":
                    act.wait_ge(dve_max, st[1] + 1)
                    nc.scalar.activation(expo[:, :], bank_L(l_use[st])[:, 0:E], ACT.Exp, bias=nmax[:, 1:2],
                                         scale=SCORE_SCALE, accum_out=esum[:, 0:1]).then_inc(act_exp, 1)
                elif kind == "B":
                    n, i = sg_use[st], b_use[st]
                    act.wait_ge(pe_SG, n + 1)
                    g = psSG[:, n % SGR, b_cols(st)]
                    nc.scalar.activation(g, g, ACT.Silu).then_inc(act_silu, 1)
                    if i:
                        store(b_order[i - 1])
                    if i + 1 < len(res_use):
                        load_res(i + 1)
            store(b_order[-1])
            for i in range(TRING):
                act.wait_ge(stored[i], 16 * len([st for st in b_order if a_use[st[1:4]] % TRING == i]))

        @block.vector
        def _(dve):
            own = [0]

            def mine(ins):
                own[0] += 1
                ins.then_inc(dve_own, 1)
                dve.wait_ge(dve_own, own[0])

            for st in steps:
                kind = st[0]
                if kind == "X":
                    n = x_use[st]
                    s, tile = n % STAT, place[st][0]
                    wait_place(dve, st)
                    for half in range(2):
                        ins = nc.vector.bn_stats(stats[:, s, half, :], tile[:, half * H:(half + 1) * H])
                    mine(ins)
                    mine(nc.vector.bn_aggr(mv[:, s, :], stats[:, s, :, :]))
                    if n >= STAT:
                        dve.wait_ge(pool_xn, n - STAT + 1)
                    nc.vector.tensor_scalar(nmean[:, s:s + 1], mv[:, s, 0:1], -1.0, None, ALU.mult)
                    nc.vector.tensor_scalar(rstd[:, s:s + 1], mv[:, s, 1:2], EPS, None, ALU.add).then_inc(dve_var, 1)
                elif kind in "TW" or kind == "D" and made_by_pe(st):
                    for half in range(1 if kind == "D" else 2):
                        n = t_use[st + (half,)]
                        hi, lo = split_target(st, half)
                        dve.wait_ge(act_T, n + 1)
                        nc.vector.tensor_tensor(lo, blocks_T(n), hi.bitcast(F32), ALU.subtract).then_inc(dve_T, 1)
                elif kind == "R":
                    m = ("M",) + st[1:]
                    w = m_use[m]
                    wait_place(dve, m)
                    if w >= 2:
                        dve.wait_ge(pe_L, l_use[list(m_use)[w - 2]] + 1)
                    nc.vector.tensor_reduce(rowcnt[:, w % 2, :], place[m][0].rearrange("p (c k) -> p c k", k=BLK),
                                            AX.X, ALU.add).then_inc(dve_cnt, 1)
                elif kind == "N":
                    m = ("M",) + st[1:]
                    n, w = l_use[m], m_use[m]
                    if w >= 2:
                        wait_masked(dve, *list(m_use)[w - 2][1:])
                    dve.wait_ge(pe_L, n + 1)
                    nc.vector.tensor_scalar(bmask[:, w % 2, :], bank_L(n)[:, 0:N // BLK], 0.0, None, ALU.is_gt)\
                        .then_inc(dve_L, 1)
                elif kind == "V" and masked_by_dve(*st[1:]):
                    m, w = ("M",) + st[1:], ("W",) + st[1:]
                    tile = place[w][0].rearrange("p (c k) -> p c k", k=BLK)
                    wait_place(dve, w)
                    dve.wait_ge(dve_L, l_use[m] + 1)
                    nc.vector.tensor_tensor(tile, tile, block_mask(m_use[m]), ALU.mult).then_inc(dve_w, 1)
                elif kind == "K":
                    n = l_use[st]
                    dve.wait_ge(pe_L, n + 1)
                    nc.vector.tensor_copy(keysT[:, :], bank_L(n)[:, 0:E]).then_inc(dve_L, 1)
                elif kind == "Q":
                    n = l_use[st]
                    dve.wait_ge(pe_L, n + 1)
                    nc.vector.tensor_copy(kq[:, :, 4 * st[1]:4 * st[1] + 4].rearrange("p e q -> p q e"),
                                          bank_L(n)[:, 0:4 * E].rearrange("p (q e) -> p q e", q=4))\
                        .then_inc(dve_L, 1)
                elif kind == "C":
                    b = st[1]
                    if b:
                        dve.wait_ge(pe_L, l_use[("G", b - 1)] + 1)
                    dve.wait_ge(act_T, t_use[("T", b, NT - 1, 1)] + 1)
                    dve.wait_ge(dve_L, l_use[("Q", 1)] + 1)
                    mine(nc.vector.tensor_reduce(xsum[:, :], xpart[:, :, :], AX.X, ALU.add))
                    mine(nc.vector.tensor_tensor(kqx[:, :, :], kq[:, :, :],
                                                 xsum[:, :].rearrange("p (o k) -> p o k", o=1).to_broadcast([P, E, KC]),
                                                 ALU.mult))
                    nc.vector.tensor_reduce(kqs[:, :], kqx[:, :, :], AX.X, ALU.add).then_inc(dve_kq, 1)
                elif kind == "G":
                    b, n = st[1], l_use[st]
                    dve.wait_ge(pe_L, n + 1)
                    mine(nc.vector.tensor_reduce(nmax[:, 0:1], bank_L(n)[:, 0:E], AX.X, ALU.max))
                    nc.vector.tensor_scalar(nmax[:, 1:2], nmax[:, 0:1], -SCORE_SCALE, None, ALU.mult)\
                        .then_inc(dve_max, 1)
                    dve.wait_ge(act_exp, b + 1)
                    mine(nc.vector.reciprocal(esum[:, 1:2], esum[:, 0:1]))
                    if b:
                        dve.wait_ge(act_U, u_use[("U", b - 1, 1, 3)] + 1)
                    pairs = expo[:, :].rearrange("p (t two) -> p two t", two=2)
                    for half in range(2):
                        rows = slice(half * R, (half + 1) * R)
                        nc.vector.tensor_scalar(coef[rows, :], pairs[rows, half, :], esum[rows, 1:2], None, ALU.mult)\
                            .then_inc(dve_coef if half else dve_L, 1)
                elif kind == "U":
                    _, b, h, t = st
                    dve.wait_ge(act_U, u_use[st] + 1)
                    nc.vector.scalar_tensor_tensor(up_lo[:, t, :], up_raw[:, t, :], coef[:, t:t + 1],
                                                   up_hi[:, t, :].bitcast(F32), ALU.mult, ALU.subtract)\
                        .then_inc(dve_U, 1)
                elif kind == "L":
                    _, b, h, k = st
                    n = l_use[st]
                    if b == 0:
                        worgT, o = stage_slot(("O", h, k)), t_use[("O", h, k, 0)]
                        dve.wait_ge(act_T, o + 1)
                    else:
                        worgT = stage_slot(st)
                        wait_stage(dve, st)
                    dve.wait_ge(pe_L, n + 1)
                    nc.vector.tensor_tensor(bank_L(n), bank_L(n), worgT, ALU.add).then_inc(dve_sum, 1)
                    dve.wait_ge(act_L, e_use[st] + 1)
                    nc.vector.tensor_tensor(e[:, 1, k, :], bank_L(n), e[:, 0, k, :].bitcast(F32), ALU.subtract)\
                        .then_inc(dve_L, 1)
                elif kind == "A" and a_part(st)[2]:
                    b, h, j = st[1:4]
                    n, a = sg_use[("A", b, h, j)], a_use[(b, h, j)]
                    if j == 0:
                        dve.wait_ge(bias_loaded, 16 * (2 * b + h + 1))
                    if a >= TRING:
                        dve.wait_ge(stored[a % TRING], 16 * (a // TRING))
                    dve.wait_ge(pe_SG, n + 1)
                    nc.vector.tensor_tensor(t_out[:, a % TRING, :], psSG[:, n % SGR, :],
                                            bias_bc[:, :], ALU.add).then_inc(dve_SG, 1)
                elif kind == "B":
                    b, h, j = st[1:4]
                    n, a, cols = sg_use[st], a_use[(b, h, j)], b_cols(st)
                    dve.wait_ge(dve_SG, sg_use[("A", b, h, j)] + 1)
                    dve.wait_ge(act_silu, b_use[st] + 1)
                    t = t_out[:, a % TRING, cols]
                    nc.vector.tensor_tensor(t, t, psSG[:, n % SGR, cols], ALU.mult).then_inc(dve_SG, 1)
                    if st == last_b:
                        i = res_use[(b, h, j)]
                        dve.wait_ge(res_loaded[i % RES], 16 * (i // RES + 1))
                        dve.wait_ge(dve_SG, n + 1)
                        nc.vector.tensor_tensor(t, t, res[:, i % RES, cols], ALU.add).then_inc(dve_out, 1)

        @block.gpsimd
        def _(pool):
            nc.gpsimd.memset(neg_half[:, :], -0.5).then_inc(consts_zeroed, 1)
            nc.gpsimd.memset(ident[:, :], 0.0).then_inc(consts_zeroed, 1)
            nc.gpsimd.memset(blk_ones[:, :], 1.0).then_inc(consts_zeroed, 1)
            nc.gpsimd.memset(ones[:, :], 1.0).then_inc(consts_ready, 1)
            pool.wait_ge(consts_zeroed, 3)
            nc.gpsimd.affine_select(out=ident[:, :], in_=ident[:, :], compare_op=ALU.not_equal, fill=1.0,
                                    base=0, pattern=[[-1, P]], channel_multiplier=1).then_inc(consts_ready, 1)
            v = blk_ones[:, :].rearrange("p (g c) -> p g c", c=BLK)
            nc.gpsimd.affine_select(out=v, in_=v, compare_op=ALU.is_ge, fill=0.0, base=0,
                                    pattern=[[-BLK, P // BLK], [0, BLK]], channel_multiplier=1)\
                .then_inc(consts_zeroed, 1)
            pool.wait_ge(consts_zeroed, 4)
            nc.gpsimd.affine_select(out=v, in_=v, compare_op=ALU.is_ge, fill=0.0, base=BLK - 1,
                                    pattern=[[BLK, P // BLK], [0, BLK]], channel_multiplier=-1)\
                .then_inc(consts_ready, 1)
            for st in steps:
                kind = st[0]
                if kind == "X":
                    n = x_use[st]
                    s = n % STAT
                    pool.wait_ge(dve_var, n + 1)
                    nc.gpsimd.tensor_tensor(rstd[:, s:s + 1], rstd[:, s:s + 1], neg_half[:, :], ALU.pow)\
                        .then_inc(pool_rstd, 1)
                elif kind == "Y":
                    n = x_use[("X",) + st[1:]]
                    s, tile = n % STAT, place[("X",) + st[1:]][0]
                    pool.wait_ge(pool_rstd, n + 1)
                    nc.gpsimd.tensor_scalar(tile, tile, nmean[:, s:s + 1], rstd[:, s:s + 1], ALU.add, ALU.mult)\
                        .then_inc(pool_xn, 1)
                elif kind == "V" and not masked_by_dve(*st[1:]):
                    m, w = ("M",) + st[1:], ("W",) + st[1:]
                    tile = place[w][0].rearrange("p (c k) -> p c k", k=BLK)
                    wait_place(pool, w)
                    pool.wait_ge(dve_L, l_use[m] + 1)
                    nc.gpsimd.tensor_tensor(tile, tile, block_mask(m_use[m]), ALU.mult).then_inc(pool_w, 1)
                elif kind == "B" and st != last_b:
                    a, i, cols = a_use[st[1:4]], res_use[st[1:4]], b_cols(st)
                    pool.wait_ge(res_loaded[i % RES], 16 * (i // RES + 1))
                    pool.wait_ge(dve_SG, sg_use[st] + 1)
                    t = t_out[:, a % TRING, cols]
                    nc.gpsimd.tensor_tensor(t, t, res[:, i % RES, cols], ALU.add).then_inc(pool_out, 1)


_INS = ["L0_attn_data", "L0_attn_mask", "L0_attn_weight", "L0_attn_bias", "L0_ffn_W_org", "L0_ffn_lora_down",
        "L0_ffn_lora_up", "L0_ffn_lora_keys", "L0_ffn_Wq"]


def kernel(**inputs):
    import numpy as _np
    import concourse.bacc as _bacc
    from concourse import mybir as _mybir
    from concourse.bass_utils import run_bass_kernel_spmd as _run

    nc = _bacc.Bacc("TRN2", target_bir_lowering=False, num_devices=1, dynamic_dma_scratch_size=1024)
    arrays, args = {}, []
    for name in _INS:
        a = _np.ascontiguousarray(inputs[name])
        arrays[f"in_{name}_dram"] = a
        args.append(nc.dram_tensor(f"in_{name}_dram", a.shape, _mybir.dt.from_np(a.dtype), kind="ExternalInput").ap())
    shape = inputs["L0_attn_data"].shape
    args.append(nc.dram_tensor("out_dram", shape, F32, kind="ExternalOutput").ap())
    gated_block_linear_lora(nc, *args)
    r = _run(nc, [arrays], core_ids=[0])
    return r.results[0]["out_dram"]
```
